# Optimizing a Trainium2 kernel written in Bass

```python
import numpy as np
import jax
import jax.numpy as jnp

def _softmax(x, axis=-1):
    return jax.nn.softmax(x, axis=axis)

def _gelu(x):
    return jax.nn.gelu(x, approximate=True)

def _silu(x):
    return jax.nn.silu(x)

def _sigmoid(x):
    return jax.nn.sigmoid(x)

def _layernorm(x, axis=-1, eps=1e-05):
    m = jnp.mean(x, axis=axis, keepdims=True)
    v = jnp.var(x, axis=axis, keepdims=True)
    return (x - m) / jnp.sqrt(v + eps)

def _scatter_add(tgt, idx, src, axis=0):
    return tgt.at[idx].add(src)

def _segment_sum(src, seg, n):
    return jax.ops.segment_sum(src, seg, n)
kernel_name = 'mk_gnn_preln_d2_gnn_r8_34bba2'

def setup_inputs(seed: int=0):
    np.random.seed(seed)
    _w = jnp.asarray

    def _rec_inputs():
        import jax
        import jax.numpy as jnp
        _gk = jax.random.key(seed)
        x = -0.0005121 + 1.001 * jax.random.normal(jax.random.fold_in(_gk, 1), (12500, 64), jnp.float32)
        _s = jax.random.randint(jax.random.fold_in(_gk, 2), (200000,), 0, 12500, jnp.int32)
        _d = jax.random.randint(jax.random.fold_in(_gk, 3), (200000,), 0, 12500, jnp.int32)
        _loop = jnp.arange(12500, dtype=jnp.int32)
        src = jnp.concatenate([_s, _d, _loop])
        dst = jnp.concatenate([_d, _s, _loop])
        _o = jnp.argsort(dst, stable=True)
        src = src[_o]
        dst = dst[_o]
        edge_attr_32 = 0.000216709 + 1.00012 * jax.random.normal(jax.random.fold_in(_gk, 12), (412500, 32), jnp.float32)
        return (x, src, dst, edge_attr_32)
    x, src, dst, edge_attr_32 = _rec_inputs()

    def _L0_gnn_setup():
        import jax, jax.numpy as jnp
        import numpy as np
        N_NODES = 6250
        N_EDGES = 100000
        D_NODE = 64
        D_EDGE = 32
        D_HID = 128

        def _mlp(x, W1, b1, W2, b2):
            return jax.nn.relu(x @ W1 + b1) @ W2 + b2
        key = jax.random.key(seed)
        ks = jax.random.split(key, 12)
        inp = {'nodes': jax.random.normal(ks[0], (N_NODES, D_NODE), dtype=jnp.float32), 'row': jax.random.randint(ks[1], (N_EDGES,), 0, N_NODES, dtype=jnp.int32), 'col': jax.random.randint(ks[2], (N_EDGES,), 0, N_NODES, dtype=jnp.int32), 'edge_features': jax.random.normal(ks[3], (N_EDGES, D_EDGE), dtype=jnp.float32)}
        d_in_msg = 2 * D_NODE + D_EDGE
        inp['mW1'] = jax.random.normal(ks[4], (d_in_msg, D_HID), dtype=jnp.float32) / np.sqrt(d_in_msg)
        inp['mb1'] = jnp.zeros((D_HID,), dtype=jnp.float32)
        inp['mW2'] = jax.random.normal(ks[5], (D_HID, D_NODE), dtype=jnp.float32) / np.sqrt(D_HID)
        inp['mb2'] = jnp.zeros((D_NODE,), dtype=jnp.float32)
        d_in_upd = 2 * D_NODE
        inp['uW1'] = jax.random.normal(ks[6], (d_in_upd, D_HID), dtype=jnp.float32) / np.sqrt(d_in_upd)
        inp['ub1'] = jnp.zeros((D_HID,), dtype=jnp.float32)
        inp['uW2'] = jax.random.normal(ks[7], (D_HID, D_NODE), dtype=jnp.float32) / np.sqrt(D_HID)
        inp['ub2'] = jnp.zeros((D_NODE,), dtype=jnp.float32)
        return inp
    _L0_gnn_all = _L0_gnn_setup()
    _L0_gnn_in = {k: v for k, v in _L0_gnn_all.items() if k in ('mW1', 'mb1', 'mW2', 'mb2', 'uW1', 'ub1', 'uW2', 'ub2')}
    del _L0_gnn_all

    def _L1_gnn_setup():
        import jax, jax.numpy as jnp
        import numpy as np
        N_NODES = 12500
        N_EDGES = 150000
        D_FEAT = 64
        key = jax.random.key(seed)
        k1, k2, k3 = jax.random.split(key, 3)
        h = jax.random.normal(k1, (N_NODES, D_FEAT), dtype=jnp.float32)
        edge_src = jax.random.randint(k2, (N_EDGES,), 0, N_NODES, dtype=jnp.int32)
        edge_dst = jax.random.randint(k3, (N_EDGES,), 0, N_NODES, dtype=jnp.int32)
        return {'h': h, 'edge_src': edge_src, 'edge_dst': edge_dst}
    _L1_gnn_all = _L1_gnn_setup()
    _L1_gnn_in = {k: v for k, v in _L1_gnn_all.items() if k in ()}
    del _L1_gnn_all
    return {'x': x, 'src': src, 'dst': dst, 'edge_attr_32': edge_attr_32, 'L0_gnn_mW1': _L0_gnn_in['mW1'], 'L0_gnn_mb1': _L0_gnn_in['mb1'], 'L0_gnn_mW2': _L0_gnn_in['mW2'], 'L0_gnn_mb2': _L0_gnn_in['mb2'], 'L0_gnn_uW1': _L0_gnn_in['uW1'], 'L0_gnn_ub1': _L0_gnn_in['ub1'], 'L0_gnn_uW2': _L0_gnn_in['uW2'], 'L0_gnn_ub2': _L0_gnn_in['ub2']}

def reference(x, src, dst, edge_attr_32, L0_gnn_mW1, L0_gnn_mb1, L0_gnn_mW2, L0_gnn_mb2, L0_gnn_uW1, L0_gnn_ub1, L0_gnn_uW2, L0_gnn_ub2):
    import jax
    import jax.numpy as jnp

    def _L0_gnn_ref(nodes, row, col, edge_features, mW1, mb1, mW2, mb2, uW1, ub1, uW2, ub2):
        import jax, jax.numpy as jnp
        import numpy as np
        N_NODES = 6250
        N_EDGES = 100000
        D_NODE = 64
        D_EDGE = 32
        D_HID = 128

        def _mlp(x, W1, b1, W2, b2):
            return jax.nn.relu(x @ W1 + b1) @ W2 + b2
        msg_in = jnp.concatenate([nodes[row], nodes[col], edge_features], axis=-1)
        messages = _mlp(msg_in, mW1, mb1, mW2, mb2)
        aggregated = jax.ops.segment_sum(messages, col, num_segments=nodes.shape[0])
        upd_in = jnp.concatenate([nodes, aggregated], axis=-1)
        return _mlp(upd_in, uW1, ub1, uW2, ub2)

    def _L1_gnn_ref(h, edge_src, edge_dst):
        import jax, jax.numpy as jnp
        import numpy as np
        N_NODES = 12500
        N_EDGES = 150000
        D_FEAT = 64
        'LightGCN propagation: h_out[v] = sum_{(u,v) in E} h[u] / sqrt(deg_out(u)*deg_in(v)).'
        n = h.shape[0]
        ones = jnp.ones(edge_src.shape[0], dtype=h.dtype)
        deg_out = jnp.maximum(jax.ops.segment_sum(ones, edge_src, num_segments=n), 1.0)
        deg_in = jnp.maximum(jax.ops.segment_sum(ones, edge_dst, num_segments=n), 1.0)
        inv_sqrt_out = jax.lax.rsqrt(deg_out)
        inv_sqrt_in = jax.lax.rsqrt(deg_in)
        w = inv_sqrt_out[edge_src] * inv_sqrt_in[edge_dst]
        m = h[edge_src] * w[:, None]
        h_out = jax.ops.segment_sum(m, edge_dst, num_segments=n)
        return h_out
    h = jnp.maximum(_layernorm(x, axis=-1), 0.0)
    x = x + _L0_gnn_ref(h, src, dst, edge_attr_32, L0_gnn_mW1, L0_gnn_mb1, L0_gnn_mW2, L0_gnn_mb2, L0_gnn_uW1, L0_gnn_ub1, L0_gnn_uW2, L0_gnn_ub2)
    h = jnp.maximum(_layernorm(x, axis=-1), 0.0)
    x = x + _L1_gnn_ref(h, src, dst)
    return x

_drawn_inputs = setup_inputs


def setup_inputs(seed=0):
    import zlib

    import numpy as np

    out = dict(_drawn_inputs(seed))
    spreads = {'L0_gnn_mb1': (0.0, 0.1),
     'L0_gnn_mb2': (0.0, 0.1),
     'L0_gnn_ub1': (0.0, 0.737),
     'L0_gnn_ub2': (0.0, 0.57)}
    factors = {}
    for name, (base, spread) in spreads.items():
        noise = np.random.default_rng([zlib.crc32(name.encode()), seed]).standard_normal(out[name].shape)
        drawn = base * np.exp(spread * noise) if base else spread * noise
        out[name] = jnp.asarray(drawn.astype(out[name].dtype))
    for name, factor in factors.items():
        out[name] = (out[name] * factor).astype(out[name].dtype)
    return out
```

```python
from contextlib import ExitStack

import numpy as np

import concourse.bass as bass
from concourse import mybir

F32 = mybir.dt.float32
BF16 = mybir.dt.bfloat16
U8 = mybir.dt.uint8
I32 = mybir.dt.int32
ALU = mybir.AluOpType
ACT = mybir.ActivationFunctionType
AX = mybir.AxisListType

P = 128
TILES = 8
GROUP = P * TILES
RING = 4
WINDOW = 64
CHUNK = 3
SLOTS = 3
EPS = 1e-5


def padded_sizes(n_nodes, n_edges):
    per = CHUNK * SLOTS
    tiles = -(-(n_nodes + WINDOW) // P)
    groups = -(-n_edges // GROUP)
    return -(-tiles // per) * per, -(-groups // RING) * RING


def bass_preln_mpnn_lightgcn(nc, x_t, src_t, dst_t, ea_t, mW1, mb1, mW2, mb2, uW1, ub1, uW2, ub2, out_t,
                             n_nodes):
    _, NT, D = x_t.shape
    T = src_t.shape[1]
    NG = T // TILES
    NI = NG // RING
    De = ea_t.shape[0]
    H = mW1.shape[1]
    NP = NT * P
    NCH = NT // CHUNK // SLOTS
    CW = CHUNK * P
    assert H == P and D + D + De == mW1.shape[0] and D == WINDOW and WINDOW + De <= P
    assert NT <= P

    table_a = nc.dram_tensor("table_a", (NP, H), F32).ap()
    table_b = nc.dram_tensor("table_b", (NP, H), F32).ap()
    table_h = nc.dram_tensor("table_h", (NP, D), F32).ap()
    ht_dram = nc.dram_tensor("ht_dram", (D, NP), F32).ap()
    sums = [nc.dram_tensor("sums_0", (NP + P, H + 1), F32).ap(),
            nc.dram_tensor("sums_1", (NP + P, D), F32).ap()]

    with ExitStack() as ctx:
        def sb(name, shape, dt=F32):
            return ctx.enter_context(nc.sbuf_tensor(name, shape, dt))

        def ps(name, banks):
            return ctx.enter_context(nc.psum_tensor(name, [P, banks * 512], F32))

        def sem(name):
            return ctx.enter_context(nc.semaphore(name))

        x = sb("x", [P, NT, D])
        work = sb("work", [P, 2 * RING * TILES * P])
        table = sb("table", [P, 2, NP])
        dst_rel = sb("dst_rel", [P, T + TILES], U8)
        src_hi = sb("src_hi", [P, T + TILES], U8)
        src_lo = sb("src_lo", [P, T + TILES], U8)
        bases = sb("bases", [1, NG + 2], I32)
        idx = sb("idx", [P, RING, TILES], I32)
        rhs = sb("rhs", [P, RING, H])
        sel = sb("sel", [P, RING, TILES, WINDOW])
        sel_b = sb("sel_b", [P, RING, TILES, WINDOW], BF16)
        hot_hi = sb("hot_hi", [P, 2, TILES, NT], BF16)
        hot_lo = sb("hot_lo", [P, 2, TILES, P], BF16)
        hid = sb("hid", [P, 2, TILES, H])
        ident = sb("ident", [P, P])
        ident_b = sb("ident_b", [P, P], BF16)
        ones = sb("ones", [P, P])
        ones_b = sb("ones_b", [P, P], BF16)
        iota_i = sb("iota_i", [P, P], I32)
        iota_f = sb("iota_f", [P, P])
        iota_b = sb("iota_b", [P, P], BF16)
        w1ab = sb("w1ab", [D + 1, 2 * H])
        w2 = sb("w2", [H, D])
        u1a = sb("u1a", [D, H])
        u1b = sb("u1b", [D, H])
        u2 = sb("u2", [H, D])
        mb2_c = sb("mb2_c", [D, 1])
        ub1_c = sb("ub1_c", [H, 1])
        ub2_r = sb("ub2_r", [1, D])
        mean = sb("mean", [P, NT])
        rstd = sb("rstd", [P, NT])
        inv_out = sb("inv_out", [P, NT])
        zero_r = sb("zero_r", [1, P])
        eps_c = sb("eps_c", [P, 1])
        small = sb("small", [P, 8])
        flag_i = sb("flag_i", [1, 1], I32)

        h = work[:, 0:NT * D].rearrange("p (t d) -> p t d", d=D)
        square = table[:, 0, 0:NT * D].rearrange("p (t d) -> p t d", d=D)
        src_i = table[:, 1, 0:T].bitcast(I32)
        dst_i = table[:, 1, T:2 * T].bitcast(I32)
        dst_f = table[:, 0, 0:T]
        shifted = table[:, 1, 2 * T:3 * T].bitcast(I32)
        gathered = work[:, 0:RING * GROUP].rearrange("p (r j f) -> p r j f", r=RING, j=TILES)
        lhs = work[:, RING * GROUP:2 * RING * GROUP].rearrange("p (r e) -> p r e", r=RING)
        gathered_h = work[:, 0:RING * TILES * D].rearrange("p (r j f) -> p r j f", r=RING, j=TILES)
        htc = hid[:, :, :, :].rearrange("p a j f -> p (a j f)")[0:D + 1, 0:SLOTS * CW].rearrange(
            "p (s n) -> p s n", s=SLOTS)
        abc = table[:, 0, 0:SLOTS * CHUNK * 2 * H].rearrange("p (s c f) -> p s c f", s=SLOTS, c=CHUNK)
        mtc = hid[:, :, :, :].rearrange("p a j f -> p (a j f)")[0:D, 0:CW]
        utc = sel[:, :, :, :].rearrange("p a j n -> p (a j n)")[:, 0:CW]
        h_stage = work[:, NT * D:NT * D + SLOTS * CHUNK * D].rearrange("p (s c f) -> p s c f", s=SLOTS, c=CHUNK)
        fin_stage = work[0:D, 0:SLOTS * CW].rearrange("p (s n) -> p s n", s=SLOTS)
        hl = work[:, 0:SLOTS * CW].rearrange("p (s n) -> p s n", s=SLOTS)[0:D]

        ps_t = ps("ps_t", 1)
        ps_selt = ctx.enter_context(nc.psum_tensor("ps_selt", [P, GROUP], BF16))
        ps_pre = [ps("ps_pre0", 2), ps("ps_pre1", 2)]
        ps_agg = ps("ps_agg", 1)
        ps_deg = ps("ps_deg", 1)
        ps_sums = [ps_agg, ps_t]

        ld_idx = sem("ld_idx")
        ld_x = sem("ld_x")
        ld_w = sem("ld_w")
        const_made = sem("const_made")
        pool_step = sem("pool_step")
        dve_step = sem("dve_step")
        viol_ready = sem("viol_ready")
        viol_t = sem("viol_t")
        flag_ready = sem("flag_ready")
        var_ready = sem("var_ready")
        std_ready = sem("std_ready")
        h_ready = sem("h_ready")
        table_clear = sem("table_clear")
        np_h = sem("np_h")
        np_t = sem("np_t")
        np_tc = sem("np_tc")
        np_mm = sem("np_mm")
        np_c = sem("np_c")
        np_st = [sem(f"np_st{k}") for k in range(SLOTS)]
        ld_grp = [sem(f"ld_grp{q}") for q in range(RING)]
        ld_src = [sem(f"ld_src{q}") for q in range(RING)]
        gat = [sem(f"gat{q}") for q in range(RING)]
        sel_ready = sem("sel_ready")
        selb_ready = sem("selb_ready")
        selt_done = sem("selt_done")
        selt_copied = sem("selt_copied")
        hot_ready = sem("hot_ready")
        hist_done = sem("hist_done")
        pre_done = sem("pre_done")
        summed = sem("summed")
        hid_ready = sem("hid_ready")
        agg_done = sem("agg_done")
        added = sem("added")
        zero_made = sem("zero_made")
        zero_st = sem("zero_st")
        gen = [{n: sem(f"gen{L}_{n}") for n in ("ld", "dstf", "gat", "dstt", "eadot", "sel", "row", "comb", "combc",
                                                "scat", "free", "hot", "hist", "fold_ld", "fold_diag", "fold_t", "fold_c")}
               for L in range(2)]
        edges_done = sem("edges_done")
        hist_closed = sem("hist_closed")
        nu_ld = [sem(f"nu_ld{k}") for k in range(SLOTS)]
        nu_m = sem("nu_m")
        nu_mc = sem("nu_mc")
        nu_u = sem("nu_u")
        nu_uc = sem("nu_uc")
        nu_y = sem("nu_y")
        nu_x = sem("nu_x")
        deg_ready = sem("deg_ready")
        deg_root = sem("deg_root")
        st_h = sem("st_h")
        ld_src1 = [sem(f"ld_src1_{q}") for q in range(RING)]
        gat1 = [sem(f"gat1_{q}") for q in range(RING)]
        sel1_ready = sem("sel1_ready")
        agg1_done = sem("agg1_done")
        added1 = sem("added1")
        edges1_done = sem("edges1_done")
        in_ready = sem("in_ready")
        in_root = sem("in_root")
        fin_scaled = sem("fin_scaled")
        fin_t = sem("fin_t")
        fin_x = sem("fin_x")
        st_out = sem("st_out")

        def load_flag(eng):
            eng.wait_ge(flag_ready, 1)
            return eng.value_load(flag_i[0:1, 0:1], min_val=0, max_val=1)

        block = ctx.enter_context(nc.Block())

        @block.sync
        def _(sp):
            sp.dma_start(dst_i, dst_t).then_inc(ld_idx, 16)
            sp.dma_start(src_i, src_t).then_inc(ld_idx, 16)
            sp.dma_start(x[:], x_t).then_inc(ld_x, 16)
            sp.dma_start(w1ab[0:D, 0:H], mW1[0:D, :]).then_inc(ld_w, 16)
            sp.dma_start(w1ab[0:D, H:2 * H], mW1[D:2 * D, :]).then_inc(ld_w, 16)
            sp.dma_start(w1ab[D:D + 1, H:2 * H], mb1.rearrange("(a f) -> a f", a=1)).then_inc(ld_w, 16)
            for q in range(RING):
                sp.dma_start(rhs[WINDOW:WINDOW + De, q, :], mW1[2 * D:2 * D + De, :]).then_inc(ld_w, 16)
            sp.dma_start(w2[:], mW2).then_inc(ld_w, 16)
            sp.dma_start(u1a[:], uW1[0:D, :]).then_inc(ld_w, 16)
            sp.dma_start(u1b[:], uW1[D:2 * D, :]).then_inc(ld_w, 16)
            sp.dma_start(u2[:], uW2).then_inc(ld_w, 16)
            sp.dma_start(mb2_c[:], mb2.rearrange("(f a) -> f a", a=1)).then_inc(ld_w, 16)
            sp.dma_start(ub1_c[:], ub1.rearrange("(f a) -> f a", a=1)).then_inc(ld_w, 16)
            sp.dma_start(ub2_r[:], ub2.rearrange("(a f) -> a f", a=1)).then_inc(ld_w, 16)

            a_rows = table_a.rearrange("(t p) f -> p t f", p=P)
            b_rows = table_b.rearrange("(t p) f -> p t f", p=P)
            with sp.Fori(0, NCH) as i:
                for k in range(SLOTS):
                    c = i * SLOTS + k
                    sp.wait_ge(np_c, c + 2)
                    sp.dma_start(a_rows[:, bass.ds(c * CHUNK, CHUNK), :], abc[:, k, :, 0:H]).then_inc(np_st[k], 16)
                    sp.dma_start(b_rows[:, bass.ds(c * CHUNK, CHUNK), :], abc[:, k, :, H:2 * H]).then_inc(np_st[k], 16)
                    sp.dma_start(ht_dram[:, bass.ds(c * CW, CW)], htc[0:D, k, :]).then_inc(np_st[k], 16)
            for k in range(SLOTS):
                sp.wait_ge(np_st[k], 48 * NCH + 48)

            def group_loads():
                def operands(g, q):
                    base = sp.value_load(bases[0:1, bass.ds(g + 1, 1)], min_val=0, max_val=n_nodes)
                    sp.wait_ge(pre_done, g + 1)
                    sp.dma_start(lhs[WINDOW:WINDOW + De, q, :], ea_t[:, bass.ds(g * GROUP, GROUP)]).then_inc(ld_grp[q], 16)
                    sp.dma_start(rhs[0:WINDOW, q, :], table_b[bass.ds(base, WINDOW), :]).then_inc(ld_grp[q], 16)

                with sp.Fori(0, NI) as i:
                    for q in range(RING):
                        g = i * RING + q
                        operands(g, q)
                        sp.wait_ge(summed, g + 1)
                        sp.dma_start(idx[:, q, :], src_t[:, bass.ds(g * TILES, TILES)]).then_inc(ld_src[q], 16)
                operands(NI * RING, 0)

            def general_loads(L):
                s, width = gen[L], (H + 1, D)[L]
                zero = hid[:, 0, 0:2, :].rearrange("p j f -> p (j f)")[:, 0:width]
                rows = sums[L].rearrange("(t p) f -> p t f", p=P)
                sp.wait_ge(zero_made, L + 1)
                with sp.Fori(0, NT + 1) as t:
                    sp.dma_start(rows[:, bass.ds(t, 1), :], zero.unsqueeze(1)).then_inc(zero_st, 16)
                with sp.Fori(0, NG) as g:
                    sp.wait_ge(s["free"], g * TILES + 1)
                    sp.nop(nofuse=True)
                    sp.dma_start(idx[:, 0, :], src_t[:, bass.ds(g * TILES, TILES)]).then_inc(s["ld"], 16)
                    sp.dma_start(idx[:, 1, :], dst_t[:, bass.ds(g * TILES, TILES)]).then_inc(s["ld"], 16)
                    if L == 0:
                        sp.dma_start(lhs[WINDOW:WINDOW + De, 0, :], ea_t[:, bass.ds(g * GROUP, GROUP)]).then_inc(s["ld"], 16)
                sp.wait_ge(s["free"], NG * TILES + 1)
                with sp.Fori(0, NT) as t:
                    sp.wait_ge(s["fold_c"], t + 1)
                    sp.dma_start(gathered[:, 0, 0:2, :].rearrange("p j f -> p (j f)")[:, 0:width].unsqueeze(1),
                                 rows[:, bass.ds(t, 1), :]).then_inc(s["fold_ld"], 16)

            general = load_flag(sp)
            with sp.If(general > 0):
                general_loads(0)
            with sp.Else():
                group_loads()

            sp.wait_ge(edges_done, 1)
            with sp.Fori(0, NCH) as i:
                for k in range(SLOTS):
                    c = i * SLOTS + k
                    sp.wait_ge(nu_u, c + 1)
                    sp.dma_start(hl[:, k, :], ht_dram[:, bass.ds(c * CW, CW)]).then_inc(nu_ld[k], 16)
            sp.wait_ge(h_ready, 2)
            sp.dma_start(table_h.rearrange("(t p) f -> p t f", p=P), h).then_inc(st_h, 16)

            def source_loads():
                with sp.Fori(0, NI) as i:
                    for q in range(RING):
                        g = i * RING + q
                        sp.wait_ge(agg1_done, g + 1)
                        sp.dma_start(idx[:, q, :], src_t[:, bass.ds(g * TILES, TILES)]).then_inc(ld_src1[q], 16)

            sp.wait_ge(st_h, 16)
            general = load_flag(sp)
            with sp.If(general > 0):
                general_loads(1)
            with sp.Else():
                source_loads()

            sp.wait_ge(fin_x, NCH * SLOTS + 1)
            sp.dma_start(out_t, x[:]).then_inc(st_out, 16)
            sp.wait_ge(st_out, 16)

        @block.gpsimd
        def _(pool):
            pool.memset(ones[:], 1.0).then_inc(const_made, 1)
            pool.memset(ident[:], 0.0).then_inc(pool_step, 1)
            pool.wait_ge(pool_step, 1)
            pool.affine_select(out=ident[:], in_=ident[:], compare_op=ALU.not_equal, fill=1.0, base=0,
                               pattern=[[-1, P]], channel_multiplier=1).then_inc(const_made, 1)
            pool.iota(iota_i[:], pattern=[[1, P]], base=0, channel_multiplier=0).then_inc(const_made, 1)
            pool.memset(eps_c[:], EPS).then_inc(const_made, 1)
            pool.wait_ge(h_ready, 1)
            with pool.Fori(0, NCH) as i:
                for k in range(SLOTS):
                    c = i * SLOTS + k
                    pool.wait_ge(np_t, c + 1)
                    pool.tensor_copy(h_stage[:, k, :, :], h[:, bass.ds(c * CHUNK, CHUNK), :]).then_inc(np_h, 1)
            for k in range(SLOTS):
                pool.wait_ge(np_st[k], 48 * NCH + 48)
            pool.wait_ge(flag_ready, 1)
            pool.memset(table[:], 0.0).then_inc(table_clear, 1)

            def gathers(rows, ring, loaded, done, freed):
                with pool.Fori(0, NI) as i:
                    for q in range(RING):
                        pool.wait_ge(loaded[q], 16 * i + 16)
                        pool.wait_ge(freed, i * RING + q + 1)
                        pool.nop(nofuse=True)
                        for j in range(TILES):
                            pool.indirect_dma_start(ring[:, q, j, :], None, rows,
                                                    bass.IndirectOffsetOnAxis(ap=idx[:, q, j:j + 1], axis=0)
                                                    ).then_inc(done[q], 16)

            def general_gathers(L):
                s, width = gen[L], (H + 1, D)[L]
                pool.wait_ge(zero_st, 16 * (NT + 1) * (L + 1))
                with pool.Fori(0, NG) as g:
                    pool.wait_ge(s["ld"], (48, 32)[L] * g + (48, 32)[L])
                    pool.nop(nofuse=True)
                    for j in range(TILES):
                        if L == 0:
                            pool.indirect_dma_start(gathered[:, 0, 0, :], None, table_a,
                                                    bass.IndirectOffsetOnAxis(ap=idx[:, 0, j:j + 1], axis=0)).then_inc(s["gat"], 16)
                            pool.indirect_dma_start(gathered[:, 0, 1, :], None, table_b,
                                                    bass.IndirectOffsetOnAxis(ap=idx[:, 1, j:j + 1], axis=0)).then_inc(s["gat"], 16)
                        else:
                            pool.indirect_dma_start(gathered_h[:, 0, 0, :], None, table_h,
                                                    bass.IndirectOffsetOnAxis(ap=idx[:, 0, j:j + 1], axis=0)).then_inc(s["gat"], 16)
                        pool.wait_ge(s["combc"], g * TILES + j + 1)
                        pool.nop(nofuse=True)
                        pool.indirect_dma_start(sums[L], bass.IndirectOffsetOnAxis(ap=idx[:, 2, 0:1], axis=0),
                                                hid[:, 1, 0:2, :].rearrange("p j f -> p (j f)")[:, 0:width], None,
                                                compute_op=ALU.add).then_inc(s["scat"], 16)
                        pool.wait_ge(s["scat"], g * (16 * TILES) + 16 * j + 16)
                        pool.sem_inc(s["free"], 1)

            general = load_flag(pool)
            with pool.If(general > 0):
                general_gathers(0)
            with pool.Else():
                gathers(table_a, gathered, ld_src, gat, summed)
            pool.wait_ge(st_h, 16)
            general = load_flag(pool)
            with pool.If(general > 0):
                general_gathers(1)
            with pool.Else():
                gathers(table_h, gathered_h, ld_src1, gat1, agg1_done)
            pool.wait_ge(edges1_done, 1)
            with pool.Fori(0, NCH) as i:
                for k in range(SLOTS):
                    c = i * SLOTS + k
                    cols = bass.ds(c * CW, CW)
                    pool.wait_ge(fin_t, c + 1)
                    pool.tensor_tensor(fin_stage[:, k, :], table[0:D, 0, cols], table[0:D, 1, cols], ALU.mult).then_inc(fin_scaled, 1)

        @block.scalar
        def _(act):
            def std(n):
                act.wait_ge(var_ready, n + 1)
                act.activation(rstd[:], mean[:], ACT.Sqrt, bias=eps_c[:, 0:1], scale=1.0 / D).then_inc(std_ready, 1)

            act.wait_ge(const_made, 7)
            std(0)
            act.wait_ge(h_ready, 1)
            with act.Fori(0, NCH) as i:
                for k in range(SLOTS):
                    c = i * SLOTS + k
                    act.wait_ge(np_t, c + SLOTS + 1)
                    act.wait_ge(np_st[k], 48 * i + 48)
                    act.copy(htc[0:D, k, :], ps_t[0:D, 0:CW]).then_inc(np_tc, 1)

            def selt_copy(g, q):
                act.wait_ge(selt_done, g + 1)
                act.wait_ge(pre_done, g + 1)
                act.copy(lhs[0:WINDOW, q, :], ps_selt[0:WINDOW, 0:GROUP]).then_inc(selt_copied, 1)

            def sel_copy(g, slot):
                act.wait_ge(sel_ready, g + 1)
                act.wait_ge(agg_done, g + 1)
                act.copy(sel_b[:, slot, :, :], sel[:, slot, :, :]).then_inc(selb_ready, 1)

            def fast_hidden():
                sel_copy(0, 0)
                selt_copy(0, 0)
                with act.Fori(0, NI) as i:
                    for q in range(RING):
                        g = i * RING + q
                        sel_copy(g + 1, (q + 1) % RING)
                        selt_copy(g + 1, (q + 1) % RING)
                        act.wait_ge(summed, g + RING + 1)
                        act.activation(hid[:, q % 2, :, :], hid[:, q % 2, :, :], ACT.Relu).then_inc(hid_ready, 1)

            general = load_flag(act)
            with act.If(general > 0):
                act.nop()
            with act.Else():
                fast_hidden()

            act.wait_ge(edges_done, 1)
            with act.Fori(0, NCH) as i:
                for k in range(SLOTS):
                    c = i * SLOTS + k
                    act.wait_ge(nu_u, c + SLOTS + 1)
                    act.wait_ge(nu_y, c + 1)
                    act.activation(utc, ps_pre[1][:, 0:CW], ACT.Relu, bias=ub1_c[:, 0:1]).then_inc(nu_uc, 1)
            act.wait_ge(deg_ready, 1)
            act.activation(inv_out[:], inv_out[:], ACT.Sqrt).then_inc(deg_root, 1)
            std(1)
            act.wait_ge(in_ready, 1)
            act.activation(table[0:D, 1, :], table[0:D, 1, :], ACT.Sqrt).then_inc(in_root, 1)

        @block.vector
        def _(dve):
            steps = [0]

            def step(ins):
                steps[0] += 1
                ins.then_inc(dve_step, 1)
                dve.wait_ge(dve_step, steps[0])

            def across(column, n):
                return column.unsqueeze(2).broadcast_to([P, NT, n])

            def normalise(n, scale):
                step(dve.tensor_reduce(mean[:], x[:], AX.X, ALU.add))
                step(dve.tensor_scalar(mean[:], mean[:], 1.0 / D, None, ALU.mult))
                step(dve.tensor_tensor(h, x[:], across(mean[:], D), ALU.subtract))
                step(dve.tensor_tensor(square, h, h, ALU.mult))
                step(dve.tensor_reduce(mean[:], square, AX.X, ALU.add))
                dve.sem_inc(var_ready, 1)
                dve.wait_ge(std_ready, n + 1)
                step(dve.reciprocal(rstd[:], rstd[:]))
                if scale is not None:
                    step(dve.tensor_tensor(rstd[:], rstd[:], scale[:], ALU.mult))
                dve.scalar_tensor_tensor(h, h, 0.0, across(rstd[:], D), ALU.max, ALU.mult).then_inc(h_ready, 1)

            dve.memset(w1ab[D:D + 1, 0:H], 0.0).then_inc(const_made, 1)
            dve.memset(htc[D:D + 1, :, :], 1.0).then_inc(const_made, 1)
            dve.memset(zero_r[:], 0.0).then_inc(const_made, 1)
            dve.wait_ge(const_made, 7)
            dve.tensor_copy(iota_f[:], iota_i[:])
            dve.tensor_copy(iota_b[:], iota_i[:])
            dve.tensor_copy(ident_b[:], ident[:])
            dve.tensor_copy(ones_b[:], ones[:])
            dve.memset(dst_rel[:, T:T + TILES], 0)
            dve.memset(src_hi[:, T:T + TILES], 0)
            dve.memset(src_lo[:, T:T + TILES], 0)
            dve.memset(bases[0:1, 0:1], 0)
            dve.memset(bases[0:1, NG + 1:NG + 2], 0)
            dve.memset(small[:], 0.0)
            dve.wait_ge(ld_idx, 32)
            dve.tensor_copy(bases[0:1, 1:NG + 1], dst_i[0:1, 0:T:TILES])
            dve.tensor_copy(dst_f, dst_i)
            step(dve.tensor_scalar(shifted, src_i, 7, None, ALU.arith_shift_right))
            step(dve.tensor_copy(src_hi[:, 0:T], shifted))
            step(dve.tensor_scalar(shifted, src_i, P - 1, None, ALU.bitwise_and))
            step(dve.tensor_copy(src_lo[:, 0:T], shifted))
            dve.sem_inc(viol_ready, 1)
            dve.wait_ge(viol_t, 1)
            rel3 = dst_f.rearrange("p (g j) -> p g j", j=TILES)
            step(dve.tensor_tensor(rel3, rel3, ps_t[:, 0:NG].unsqueeze(2).broadcast_to([P, NG, TILES]), ALU.subtract))
            dve.tensor_copy(dst_rel[:, 0:T], dst_f)
            step(dve.tensor_reduce(small[:, 0:1], dst_f, AX.X, ALU.max))
            step(dve.tensor_reduce(small[:, 1:2], dst_f, AX.X, ALU.min))
            step(dve.tensor_scalar(small[:, 0:1], small[:, 0:1], float(1 - WINDOW), None, ALU.add))
            step(dve.scalar_tensor_tensor(small[:, 2:3], small[:, 1:2], -1.0, small[:, 0:1], ALU.mult, ALU.max))
            dve.sem_inc(viol_ready, 1)
            dve.wait_ge(viol_t, 2)
            step(dve.tensor_reduce(small[0:1, 3:4], ps_t[0:1, 0:P], AX.X, ALU.max))
            dve.tensor_scalar(flag_i[:], small[0:1, 3:4], 0.0, None, ALU.is_gt).then_inc(flag_ready, 1)

            dve.wait_ge(ld_x, 16)
            normalise(0, None)
            dve.wait_ge(h_ready, 1)
            with dve.Fori(0, NCH) as i:
                for k in range(SLOTS):
                    c = i * SLOTS + k
                    dve.wait_ge(np_mm, c + 1)
                    dve.wait_ge(np_st[k], 48 * i + 48)
                    dve.tensor_copy(abc[:, k, :, :], ps_pre[0][:, 0:CHUNK * 2 * H].rearrange("p (c f) -> p c f", c=CHUNK)).then_inc(np_c, 1)

            iota_w = iota_b[:, 0:WINDOW].unsqueeze(1).broadcast_to([P, TILES, WINDOW])

            def make_sel(col, slot, ready):
                rel = dst_rel[:, bass.ds(col, TILES)].unsqueeze(2).broadcast_to([P, TILES, WINDOW])
                dve.tensor_tensor(sel[:, slot, :, :], rel, iota_w, ALU.is_equal).then_inc(ready, 1)

            def make_hot(col, slot, ready):
                hi = src_hi[:, bass.ds(col, TILES)].unsqueeze(2)
                lo = src_lo[:, bass.ds(col, TILES)].unsqueeze(2)
                dve.tensor_tensor(hot_hi[:, slot, :, :], hi.broadcast_to([P, TILES, NT]),
                                  iota_b[:, 0:NT].unsqueeze(1).broadcast_to([P, TILES, NT]), ALU.is_equal).then_inc(ready, 1)
                dve.tensor_tensor(hot_lo[:, slot, :, :], lo.broadcast_to([P, TILES, P]),
                                  iota_b[:, :].unsqueeze(1).broadcast_to([P, TILES, P]), ALU.is_equal).then_inc(ready, 1)

            def add_window(base, slot, rows, halves, done, n):
                dve.wait_ge(done, n)
                spot = table[0:rows, 0:halves, bass.ds(base, WINDOW)]
                new = ps_sums[slot][0:rows, 0:halves * WINDOW].rearrange("p (a n) -> p a n", a=halves)
                dve.tensor_tensor(spot, spot, new, ALU.add).then_inc(done, 1)

            def fast_layer0():
                dve.wait_ge(table_clear, 1)
                dve.wait_ge(agg_done, 1)
                make_sel(0, 0, sel_ready)
                dve.wait_ge(hist_done, 1)
                make_hot(0, 0, hot_ready)
                with dve.Fori(0, NI) as i:
                    for q in range(RING):
                        g = i * RING + q
                        base = dve.value_load(bases[0:1, bass.ds(g, 1)], min_val=0, max_val=n_nodes)
                        dve.wait_ge(agg_done, g + 2)
                        make_sel((g + 1) * TILES, (q + 1) % RING, sel_ready)
                        dve.wait_ge(hist_done, g + 2)
                        make_hot((g + 1) * TILES, (q + 1) % 2, hot_ready)
                        dve.wait_ge(pre_done, g + RING + 1)
                        dve.wait_ge(gat[q], 16 * TILES * i + 16 * TILES)
                        dve.wait_ge(agg_done, g + 3)
                        for half in range(2):
                            t0 = half * TILES // 2
                            ins = dve.tensor_tensor(
                                hid[:, q % 2, t0:t0 + TILES // 2, :], gathered[:, q, t0:t0 + TILES // 2, :],
                                ps_pre[q % 2][:, 512 * half:512 * half + 512].rearrange("p (j f) -> p j f", f=H), ALU.add)
                        ins.then_inc(summed, 1)
                        dve.wait_ge(agg_done, g + 4)
                        add_window(base, (q + 1) % 2, P, 2, added, g + 2)
                base = dve.value_load(bases[0:1, NG:NG + 1], min_val=0, max_val=n_nodes)
                dve.wait_ge(agg_done, NG + 4)
                add_window(base, (NG + 1) % 2, P, 2, added, NG + 2)
                dve.wait_ge(added, NG + 3)

            def general_layer(L):
                s, width = gen[L], (H + 1, D)[L]
                if L == 0:
                    dve.wait_ge(table_clear, 1)
                dve.memset(hid[:, 0, 0:2, :], 0.0).then_inc(zero_made, 1)
                dve.wait_ge(zero_st, 16 * (NT + 1) * (L + 1))
                val = hid[:, 0, 0:2, :].rearrange("p j f -> p (j f)")
                out_rows = hid[:, 1, 0:2, :].rearrange("p j f -> p (j f)")[:, 0:width]
                dstf, eq, low = small[:, 4:5], gathered[:, 1, 0, :], gathered[:, 1, 1, :]
                n = [0]

                def link(ins, g, sem_name="row", per=0):
                    n[0] += 1
                    ins.then_inc(s[sem_name], 1)
                    dve.wait_ge(s[sem_name], g * per + n[0])

                per_tile = 6 if L == 0 else 4
                dve.memset(val[:, H:H + 1], 1.0).then_inc(s["row"], 1)
                dve.wait_ge(s["row"], 1)
                n[0] = 1
                with dve.Fori(0, NG) as g:
                    dve.wait_ge(s["ld"], (48, 32)[L] * g + (48, 32)[L])
                    if L == 0:
                        dve.wait_ge(s["hist"], g + 1)
                        make_hot(g * TILES, 0, s["hot"])
                    for j in range(TILES):
                        dve.wait_ge(s["dstt"], g * TILES + j + 1)
                        dve.wait_ge(s["free"], g * TILES + j + 1)
                        dve.tensor_copy(dstf, idx[:, 1, j:j + 1]).then_inc(s["dstf"], 1)
                        dve.wait_ge(s["dstf"], g * TILES + j + 1)
                        dve.wait_ge(s["dstt"], g * TILES + j + 2)
                        link(dve.tensor_scalar(eq, ps_t[:, 0:P], dstf, None, ALU.is_equal), g, "row", per_tile * TILES)
                        link(dve.scalar_tensor_tensor(low, iota_f[:, :], small[:, 5:6], eq, ALU.is_lt, ALU.mult), g, "row", per_tile * TILES)
                        link(dve.tensor_reduce(small[:, 6:7], low, AX.X, ALU.max), g, "row", per_tile * TILES)
                        link(dve.scalar_tensor_tensor(small[:, 7:8], small[:, 5:6], float(NP), dstf, ALU.add, ALU.subtract), g, "row", per_tile * TILES)
                        dve.scalar_tensor_tensor(idx[:, 2, 0:1], small[:, 7:8], small[:, 6:7], dstf, ALU.mult, ALU.add).then_inc(s["sel"], 1)
                        dve.wait_ge(s["gat"], ((32 * TILES) if L == 0 else 16 * TILES) * g + (32 if L == 0 else 16) * (j + 1))
                        if L == 0:
                            dve.wait_ge(s["eadot"], g * TILES + j + 1)
                            link(dve.tensor_tensor(gathered[:, 0, 0, :], gathered[:, 0, 0, :], gathered[:, 0, 1, :], ALU.add), g, "row", per_tile * TILES)
                            link(dve.tensor_tensor(gathered[:, 0, 0, :], gathered[:, 0, 0, :], ps_pre[0][:, 0:H], ALU.add), g, "row", per_tile * TILES)
                            dve.tensor_scalar(val[:, 0:H], gathered[:, 0, 0, :], 0.0, None, ALU.max).then_inc(s["sel"], 1)
                        dve.wait_ge(s["comb"], g * TILES + j + 1)
                        dve.tensor_copy(out_rows, ps_agg[:, 0:width]).then_inc(s["combc"], 1)
                with dve.Fori(0, NT) as t:
                    dve.wait_ge(s["fold_ld"], 16 * t + 16)
                    if L == 0:
                        dve.tensor_scalar(eq, ident[:, :], gathered[:, 0, 1, 0:1], None, ALU.mult).then_inc(s["fold_diag"], 1)
                    dve.wait_ge(s["fold_t"], t + 1)
                    if L == 0:
                        dve.tensor_copy(table[:, :, bass.ds(t * P, P)],
                                        ps_t[:, 0:2 * P].rearrange("p (a n) -> p a n", a=2)).then_inc(s["fold_c"], 1)
                    else:
                        dve.tensor_copy(table[0:D, 0, bass.ds(t * P, P)], ps_t[0:D, 0:P]).then_inc(s["fold_c"], 1)
                dve.wait_ge(s["fold_c"], NT + 1)

            dve.wait_ge(flag_ready, 1)
            dve.wait_ge(viol_t, 3)
            dve.tensor_copy(small[:, 5:6], ps_agg[:, 0:1]).then_inc(viol_ready, 1)
            dve.wait_ge(viol_ready, 3)
            general = load_flag(dve)
            with dve.If(general > 0):
                general_layer(0)
            with dve.Else():
                fast_layer0()
            dve.sem_inc(edges_done, 1)

            with dve.Fori(0, NCH) as i:
                for k in range(SLOTS):
                    c = i * SLOTS + k
                    dve.wait_ge(nu_m, c + 1)
                    dve.wait_ge(nu_u, c + SLOTS)
                    dve.scalar_tensor_tensor(mtc, table[0:D, 1, bass.ds(c * CW, CW)], mb2_c[:, 0:1], ps_pre[0][0:D, 0:CW],
                                             ALU.mult, ALU.add).then_inc(nu_mc, 1)
                    dve.wait_ge(nu_y, c + 2)
                    rows = x[:, bass.ds(c * CHUNK, CHUNK), :]
                    dve.tensor_tensor(rows, rows, ps_agg[:, 0:CHUNK * D].rearrange("p (c f) -> p c f", c=CHUNK),
                                      ALU.add).then_inc(nu_x, 1)
            dve.wait_ge(nu_x, NCH * SLOTS + 1)
            dve.wait_ge(hist_closed, 1)
            dve.tensor_scalar(inv_out[:], ps_deg[:, 0:NT], 1.0, None, ALU.max).then_inc(deg_ready, 1)
            dve.wait_ge(deg_root, 1)
            step(dve.reciprocal(inv_out[:], inv_out[:]))
            normalise(1, inv_out)
            dve.wait_ge(h_ready, 2)
            dve.memset(table[0:D, 0, :], 0.0)
            dve.tensor_scalar(table[0:D, 1, :], table[0:D, 1, :], 1.0, None, ALU.max).then_inc(in_ready, 1)

            def fast_layer1():
                dve.wait_ge(agg1_done, RING - 1)
                make_sel(0, 0, sel1_ready)
                with dve.Fori(0, NI) as i:
                    for q in range(RING):
                        g = i * RING + q
                        dve.wait_ge(agg1_done, g + RING)
                        make_sel((g + 1) * TILES, (q + 1) % 2, sel1_ready)
                        base = dve.value_load(bases[0:1, bass.ds(g + 1, 1)], min_val=0, max_val=n_nodes)
                        dve.wait_ge(agg1_done, g + RING + 1)
                        add_window(base, 0, D, 1, added1, g + 1)
                dve.wait_ge(added1, NG + 1)

            general = load_flag(dve)
            with dve.If(general > 0):
                general_layer(1)
            with dve.Else():
                fast_layer1()

            dve.wait_ge(in_root, 1)
            step(dve.reciprocal(table[0:D, 1, :], table[0:D, 1, :]))
            dve.sem_inc(edges1_done, 1)
            with dve.Fori(0, NCH * SLOTS) as c:
                dve.wait_ge(fin_t, c + SLOTS + 1)
                rows = x[:, bass.ds(c * CHUNK, CHUNK), :]
                dve.tensor_tensor(rows, rows, ps_t[:, 0:CHUNK * D].rearrange("p (c f) -> p c f", c=CHUNK),
                                  ALU.add).then_inc(fin_x, 1)

        @block.tensor
        def _(pe):
            pe.wait_ge(const_made, 7)
            pe.sem_inc(pre_done, RING)
            pe.sem_inc(summed, RING)
            pe.sem_inc(agg_done, RING - 1)
            pe.sem_inc(hist_done, 2)
            pe.sem_inc(added, 2)
            pe.sem_inc(agg1_done, RING)
            pe.sem_inc(added1, 1)
            pe.sem_inc(nu_u, SLOTS)
            pe.sem_inc(np_t, SLOTS)
            pe.sem_inc(fin_t, SLOTS)
            pe.sem_inc(nu_y, 1)
            pe.sem_inc(fin_x, 1)
            pe.sem_inc(np_tc, 1)
            pe.sem_inc(np_c, 1)
            pe.sem_inc(selt_copied, 1)
            pe.sem_inc(nu_mc, 1)
            pe.sem_inc(nu_uc, 1)
            pe.sem_inc(nu_x, 1)
            for k in range(SLOTS):
                pe.sem_inc(np_st[k], 48)
            for L in range(2):
                pe.sem_inc(gen[L]["dstt"], 1)
                pe.sem_inc(gen[L]["hist"], 1)
                pe.sem_inc(gen[L]["free"], 1)
                pe.sem_inc(gen[L]["fold_c"], 1)
            pe.wait_ge(viol_ready, 1)
            pe.matmul(ps_t[:, 0:NG], ones[0:1, :], dst_f[0:1, 0:T:TILES], start=True, stop=True).then_inc(viol_t, 1)
            pe.wait_ge(viol_ready, 2)
            pe.matmul(ps_t[0:1, 0:P], small[:, 2:3], ident[:, :], start=True, stop=True).then_inc(viol_t, 1)
            pe.matmul(ps_agg[:, 0:1], iota_f[0:1, :], ones[0:1, 0:1], start=True, stop=True).then_inc(viol_t, 1)

            pe.wait_ge(flag_ready, 1)
            pe.wait_ge(h_ready, 1)
            pe.wait_ge(ld_w, 16 * (10 + RING))
            with pe.Fori(0, NCH) as i:
                for k in range(SLOTS):
                    c = i * SLOTS + k
                    pe.wait_ge(np_h, c + 1)
                    pe.wait_ge(np_tc, c + 1)
                    pe.nop(nofuse=True)
                    for t in range(CHUNK):
                        ins = pe.transpose(ps_t[0:D, t * P:(t + 1) * P], h_stage[:, k, t, :], ident[:, :])
                    ins.then_inc(np_t, 1)
                    pe.wait_ge(np_tc, c + 2)
                    pe.wait_ge(np_c, c + 1)
                    for t in range(CHUNK):
                        ins = pe.matmul(ps_pre[0][:, t * 2 * H:(t + 1) * 2 * H], htc[:, k, t * P:(t + 1) * P], w1ab[:, :],
                                        start=True, stop=True)
                    ins.then_inc(np_mm, 1)

            def open_hist():
                pe.matmul(ps_deg[:, 0:NT], ones[0:1, :], zero_r[:, 0:NT], start=True, stop=False, skip_group_check=True)

            def hist(slot, done):
                for j in range(TILES):
                    ins = pe.matmul(ps_deg[:, 0:NT], hot_lo[:, slot, j, :], hot_hi[:, slot, j, :],
                                    start=False, stop=False, skip_group_check=True)
                ins.then_inc(done, 1)

            def sel_transposed(g, slot):
                pe.wait_ge(selb_ready, g + 1)
                pe.wait_ge(selt_copied, g + 1)
                pe.nop(nofuse=True)
                for j in range(TILES):
                    ins = pe.transpose(ps_selt[0:WINDOW, j * P:(j + 1) * P], sel_b[:, slot, j, :], ident_b[:, :])
                ins.then_inc(selt_done, 1)

            def products(g, q, trip):
                pe.wait_ge(ld_grp[q], 32 * trip + 32)
                pe.wait_ge(selt_copied, g + 2)
                pe.wait_ge(summed, g + RING - 1)
                for j in range(TILES):
                    ins = pe.matmul(ps_pre[q % 2][:, j * H:(j + 1) * H], lhs[0:WINDOW + De, q, j * P:(j + 1) * P],
                                    rhs[0:WINDOW + De, q, :], start=True, stop=True)
                ins.then_inc(pre_done, 1)

            def fast_layer0():
                pe.wait_ge(viol_ready, 3)
                pe.matmul(ps_sums[1][:, 0:2 * WINDOW], ones[0:1, :], zero_r[:, 0:2 * WINDOW], start=True, stop=True,
                          skip_group_check=True).then_inc(agg_done, 1)
                sel_transposed(0, 0)
                products(0, 0, 0)
                with pe.Fori(0, NI) as i:
                    for q in range(RING):
                        g = i * RING + q
                        sel_transposed(g + 1, (q + 1) % RING)
                        pe.wait_ge(hot_ready, 2 * g + 2)
                        hist(q % 2, hist_done)
                        products(g + 1, (q + 1) % RING, i + (q + 1) // RING)
                        pe.wait_ge(hid_ready, g + 1)
                        pe.wait_ge(added, g + 2)
                        for j in range(TILES):
                            for f in range(0, H, H // 2):
                                pe.matmul(ps_sums[q % 2][f:f + H // 2, 0:WINDOW], hid[:, q % 2, j, f:f + H // 2], sel[:, q, j, :],
                                          start=(j == 0), stop=(j == TILES - 1), skip_group_check=True)
                            ins = pe.matmul(ps_sums[q % 2][:, WINDOW:2 * WINDOW], ones_b[:, :], sel_b[:, q, j, :],
                                            start=False, stop=(j == TILES - 1), skip_group_check=True)
                        ins.then_inc(agg_done, 1)

            def general_layer(L):
                s, width = gen[L], (H + 1, D)[L]
                val = hid[:, 0, 0:2, :].rearrange("p j f -> p (j f)") if L == 0 else gathered_h[:, 0, 0, :]
                with pe.Fori(0, NG) as g:
                    pe.wait_ge(s["ld"], (48, 32)[L] * g + (48, 32)[L])
                    if L == 0:
                        pe.wait_ge(s["hot"], 2 * g + 2)
                        hist(0, s["hist"])
                    for j in range(TILES):
                        pe.wait_ge(s["dstf"], g * TILES + j + 1)
                        pe.matmul(ps_t[:, 0:P], small[:, 4:5].broadcast_to([P, P]), ident[:, :], start=True, stop=True).then_inc(s["dstt"], 1)
                        if L == 0:
                            pe.matmul(ps_pre[0][:, 0:H], lhs[WINDOW:WINDOW + De, 0, j * P:(j + 1) * P], rhs[WINDOW:WINDOW + De, 0, :],
                                      start=True, stop=True).then_inc(s["eadot"], 1)
                        pe.wait_ge(s["sel"], (2 * TILES if L == 0 else TILES) * g + (2 if L == 0 else 1) * (j + 1))
                        pe.wait_ge(s["gat"], ((32 * TILES) if L == 0 else 16 * TILES) * g + (32 if L == 0 else 16) * (j + 1))
                        pe.matmul(ps_agg[:, 0:width], gathered[:, 1, 0, :], val[:, 0:width], start=True, stop=True).then_inc(s["comb"], 1)
                with pe.Fori(0, NT) as t:
                    pe.wait_ge(s["fold_ld"], 16 * t + 16)
                    pe.nop(nofuse=True)
                    if L == 0:
                        pe.transpose(ps_t[:, 0:P], gathered[:, 0, 0, :], ident[:, :])
                        pe.wait_ge(s["fold_diag"], t + 1)
                        pe.matmul(ps_t[:, P:2 * P], ones[:, :], gathered[:, 1, 0, :], start=True, stop=True).then_inc(s["fold_t"], 1)
                    else:
                        pe.transpose(ps_t[0:D, 0:P], gathered_h[:, 0, 0, :], ident[:, :]).then_inc(s["fold_t"], 1)

            open_hist()
            general = load_flag(pe)
            with pe.If(general > 0):
                general_layer(0)
            with pe.Else():
                fast_layer0()
            pe.matmul(ps_deg[:, 0:NT], ones[0:1, :], zero_r[:, 0:NT], start=False, stop=True,
                      skip_group_check=True).then_inc(hist_closed, 1)

            pe.wait_ge(edges_done, 1)
            with pe.Fori(0, NCH) as i:
                for k in range(SLOTS):
                    c = i * SLOTS + k
                    pe.wait_ge(nu_mc, c + 1)
                    pe.matmul(ps_pre[0][0:D, 0:CW], w2[:, :], table[:, 0, bass.ds(c * CW, CW)], start=True, stop=True).then_inc(nu_m, 1)
                    pe.wait_ge(nu_ld[k], 16 * i + 16)
                    pe.wait_ge(nu_uc, c + 1)
                    pe.matmul(ps_pre[1][:, 0:CW], u1a[:, :], hl[:, k, :], start=True, stop=False)
                    pe.wait_ge(nu_mc, c + 2)
                    pe.matmul(ps_pre[1][:, 0:CW], u1b[:, :], mtc, start=False, stop=True).then_inc(nu_u, 1)
                    pe.wait_ge(nu_uc, c + 2)
                    pe.wait_ge(nu_x, c + 1)
                    for t in range(CHUNK):
                        o = ps_agg[:, t * D:(t + 1) * D]
                        pe.matmul(o, utc[:, t * P:(t + 1) * P], u2[:, :], start=True, stop=False)
                        ins = pe.matmul(o, ones[0:1, :], ub2_r[:, :], start=False, stop=True)
                    ins.then_inc(nu_y, 1)

            def fast_layer1():
                with pe.Fori(0, NI) as i:
                    for q in range(RING):
                        g = i * RING + q
                        pe.wait_ge(sel1_ready, g + 1)
                        pe.wait_ge(gat1[q], 16 * TILES * i + 16 * TILES)
                        pe.wait_ge(added1, g + 1)
                        for j in range(TILES):
                            ins = pe.matmul(ps_agg[0:D, 0:WINDOW], gathered_h[:, q, j, :], sel[:, q % 2, j, :],
                                            start=(j == 0), stop=(j == TILES - 1))
                        ins.then_inc(agg1_done, 1)

            pe.wait_ge(in_ready, 1)
            general = load_flag(pe)
            with pe.If(general > 0):
                general_layer(1)
            with pe.Else():
                fast_layer1()
            pe.wait_ge(edges1_done, 1)
            with pe.Fori(0, NCH) as i:
                for k in range(SLOTS):
                    c = i * SLOTS + k
                    pe.wait_ge(fin_scaled, c + 1)
                    pe.wait_ge(fin_x, c + 1)
                    pe.nop(nofuse=True)
                    for t in range(CHUNK):
                        ins = pe.transpose(ps_t[:, t * D:(t + 1) * D], fin_stage[:, k, t * P:(t + 1) * P], ident[0:D, 0:D])
                    ins.then_inc(fin_t, 1)


_OUT = "out_dram"


def kernel(x, src, dst, edge_attr_32, L0_gnn_mW1, L0_gnn_mb1, L0_gnn_mW2, L0_gnn_mb2, L0_gnn_uW1, L0_gnn_ub1,
           L0_gnn_uW2, L0_gnn_ub2):
    import concourse.bacc as bacc
    from concourse.bass_utils import run_bass_kernel_spmd

    x, src, dst, ea = (np.asarray(a) for a in (x, src, dst, edge_attr_32))
    n, d = x.shape
    e, de = ea.shape
    nt, ng = padded_sizes(n, e)
    x_t = np.zeros((nt * P, d), x.dtype)
    x_t[:n] = x
    x_t = np.ascontiguousarray(x_t.reshape(nt, P, d).transpose(1, 0, 2))

    def columns(a):
        p = np.full(ng * GROUP, n, a.dtype)
        p[:e] = a
        return np.ascontiguousarray(p.reshape(ng * TILES, P).T)

    ea_t = np.zeros((de, (ng + 1) * GROUP), ea.dtype)
    ea_t[:, :e] = ea.T
    arrays = {"x_t": x_t, "src_t": columns(src), "dst_t": columns(dst), "ea_t": ea_t}
    for name, w in (("mW1", L0_gnn_mW1), ("mb1", L0_gnn_mb1), ("mW2", L0_gnn_mW2), ("mb2", L0_gnn_mb2),
                    ("uW1", L0_gnn_uW1), ("ub1", L0_gnn_ub1), ("uW2", L0_gnn_uW2), ("ub2", L0_gnn_ub2)):
        arrays[name] = np.ascontiguousarray(w)
    nc = bacc.Bacc("TRN2", target_bir_lowering=False, num_devices=1)
    args = [nc.dram_tensor(k, a.shape, mybir.dt.from_np(a.dtype), kind="ExternalInput").ap() for k, a in arrays.items()]
    out = nc.dram_tensor(_OUT, x_t.shape, F32, kind="ExternalOutput").ap()
    bass_preln_mpnn_lightgcn(nc, *args, out, n)
    got = run_bass_kernel_spmd(nc, [arrays], core_ids=[0]).results[0][_OUT]
    return got.transpose(1, 0, 2).reshape(nt * P, d)[:n]
```

```python
from contextlib import ExitStack

import numpy as np

import concourse.bass as bass
from concourse import mybir

F32 = mybir.dt.float32
BF16 = mybir.dt.bfloat16
F16 = mybir.dt.float16
U8 = mybir.dt.uint8
I32 = mybir.dt.int32
ALU = mybir.AluOpType
ACT = mybir.ActivationFunctionType
AX = mybir.AxisListType

P = 128
TILES = 8
GROUP = P * TILES
RING = 4
WINDOW = 64
HALF = 2 * TILES
SPAN = 7
REACH = 96
CODES = 4
CHUNK = 3
SLOTS = 3
EPS = 1e-5


def padded_sizes(n_nodes, n_edges):
    per = CHUNK * SLOTS
    tiles = -(-(n_nodes + REACH) // P)
    groups = -(-n_edges // GROUP)
    return -(-tiles // per) * per, -(-groups // (2 * RING)) * 2 * RING


def bass_preln_mpnn_lightgcn(nc, x_t, src_t, dst_t, ea_t, mW1, mb1, mW2, mb2, uW1, ub1, uW2, ub2, out_t,
                             n_nodes, n_edges):
    _, NT, D = x_t.shape
    T = src_t.shape[1]
    NG = T // TILES
    NI = -(-n_edges // (GROUP * RING))
    N0 = NI * RING
    NI1 = NG // (2 * RING)
    NH = 2 * NI1
    G1 = NG // 2
    T1 = G1 * TILES
    HI = 2 * (n_nodes // (2 * P) + 1)
    V = HALF * SPAN
    De = ea_t.shape[0]
    H = mW1.shape[1]
    NP = NT * P
    NCH = NT // CHUNK // SLOTS
    CW = CHUNK * P
    assert H == P and D + D + De == mW1.shape[0] and D == WINDOW and WINDOW + De <= P
    assert NT <= P and HI <= NT and HI // 2 * SPAN <= 512 and V <= P

    table_a = nc.dram_tensor("table_a", (NP, H), F32).ap()
    table_b = nc.dram_tensor("table_b", (NP, H), F32).ap()
    table_h = nc.dram_tensor("table_h", (NP, D), F32).ap()
    ht_dram = nc.dram_tensor("ht_dram", (D, NP), F32).ap()
    sums = [nc.dram_tensor("sums_0", (NP + P, H + 1), F32).ap(),
            nc.dram_tensor("sums_1", (NP + P, D), F32).ap()]

    with ExitStack() as ctx:
        def sb(name, shape, dt=F32):
            return ctx.enter_context(nc.sbuf_tensor(name, shape, dt))

        def ps(name, banks):
            return ctx.enter_context(nc.psum_tensor(name, [P, banks * 512], F32))

        def sem(name):
            return ctx.enter_context(nc.semaphore(name))

        x = sb("x", [P, NT, D])
        work = sb("work", [P, max(2 * RING * TILES * P, HI * 3 * D // 2)])
        table = sb("table", [P, 2, NP])
        dst_rel = sb("dst_rel", [P, T + TILES], U8)
        src_hi = sb("src_hi", [P, T + TILES], U8)
        src_lo = sb("src_lo", [P, T + TILES], U8)
        code = sb("code", [P, T - T1 + TILES], F16)
        node_of = sb("node_of", [V, NH + 1])
        bases = sb("bases", [1, NG + 2], I32)
        idx = sb("idx", [P, RING, TILES], I32)
        rhs = sb("rhs", [P, RING, H])
        sel = sb("sel", [P, RING, TILES, WINDOW])
        sel_b = sb("sel_b", [P, 2, TILES, WINDOW], BF16)
        hot_hi = sb("hot_hi", [P, 2, TILES, NT], BF16)
        hot_lo = sb("hot_lo", [P, 2, TILES, P], BF16)
        hid = sb("hid", [P, 2, TILES, H])
        ident = sb("ident", [P, P])
        ident_b = sb("ident_b", [P, P], BF16)
        ones = sb("ones", [P, P])
        ones_b = sb("ones_b", [P, P], BF16)
        iota_f = sb("iota_f", [P, P])
        iota_b = sb("iota_b", [P, P], BF16)
        w2 = sb("w2", [H, D])
        u1a = sb("u1a", [D, H])
        u1b = sb("u1b", [D, H])
        u2 = sb("u2", [H, D])
        mb2_c = sb("mb2_c", [D, 1])
        ub1_c = sb("ub1_c", [H, 1])
        ub2_r = sb("ub2_r", [1, D])
        inv_out = sb("inv_out", [P, NT])
        zero_r = sb("zero_r", [1, P])
        eps_c = sb("eps_c", [P, 1])
        small = sb("small", [P, 16])
        flag_i = sb("flag_i", [1, 2], I32)

        sel_flat = sel[:, :, :, :].rearrange("p a j n -> p (a j n)")
        hid_flat = hid[:, :, :, :].rearrange("p a j f -> p (a j f)")
        hot_lo_f = hot_lo[:, :, :, :].rearrange("p a j n -> p (a j n)").bitcast(F32)
        mean = hot_lo_f[:, 0:NT]
        rstd = hot_lo_f[:, NT:2 * NT]
        iota_i = sel_flat[:, 0:P].bitcast(I32)
        w1ab = sel_flat[0:D + 1, P:P + 2 * H]
        tile_row = hid_flat[0:1, 0:HALF * (V + SPAN)]
        mod_row = hid_flat[0:1, HALF * (V + SPAN):HALF * (V + SPAN) + V]
        h2 = table[:, 1, 0:NT * D].rearrange("p (t d) -> p t d", d=D)
        square2 = table[:, 1, NT * D:2 * NT * D].rearrange("p (t d) -> p t d", d=D)
        parts = work[:, 0:HI * 3 * D // 2].bitcast(BF16).rearrange("p (t a d) -> p t a d", a=3, d=D)
        counts = table[:, 1, 0:HI * V].bitcast(BF16).rearrange("p (a t v) -> p a t v", a=2, t=HI)
        hot_code = table[:, 1, HI * V:HI * V + CODES * HI * SPAN // 2].bitcast(BF16).rearrange(
            "p (r c) -> p r c", r=CODES)
        ring1 = hid_flat.rearrange("p (r j f) -> p r j f", r=RING, j=TILES)
        iota_c = hot_hi[:, :, :, :].rearrange("p a j t -> p (a j t)")[:, 0:HI * SPAN].bitcast(F16)
        iota_ci = work[:, 2 * RING * TILES * P - HI * SPAN:2 * RING * TILES * P].bitcast(I32)
        summed_rows = rhs[0:V, 0, 0:D]
        code_s = rhs[:, 2, 0:2 * TILES].rearrange("p (a j) -> p a j", a=2)
        place = rhs[0:V, 1, 0:REACH]
        h = work[:, 0:NT * D].rearrange("p (t d) -> p t d", d=D)
        square = table[:, 0, 0:NT * D].rearrange("p (t d) -> p t d", d=D)
        src_i = table[:, 1, 0:T].bitcast(I32)
        dst_i = table[:, 1, T:2 * T].bitcast(I32)
        dst_f = table[:, 0, 0:T]
        rel_tile = table[:, 0, T:T + T - T1]
        rel_half = table[:, 0, 2 * T:2 * T + T - T1]
        shifted = table[:, 1, 2 * T:3 * T].bitcast(I32)
        gathered = work[:, 0:RING * GROUP].rearrange("p (r j f) -> p r j f", r=RING, j=TILES)
        lhs = work[:, RING * GROUP:2 * RING * GROUP].rearrange("p (r e) -> p r e", r=RING)
        gathered_h = work[:, 0:RING * TILES * D].rearrange("p (r j f) -> p r j f", r=RING, j=TILES)
        htc = hid[:, :, :, :].rearrange("p a j f -> p (a j f)")[0:D + 1, 0:SLOTS * CW].rearrange(
            "p (s n) -> p s n", s=SLOTS)
        abc = table[:, 0, 0:SLOTS * CHUNK * 2 * H].rearrange("p (s c f) -> p s c f", s=SLOTS, c=CHUNK)
        mtc = hid[:, :, :, :].rearrange("p a j f -> p (a j f)")[0:D, 0:CW]
        utc = sel[:, :, :, :].rearrange("p a j n -> p (a j n)")[:, 0:CW]
        h_stage = work[:, NT * D:NT * D + SLOTS * CHUNK * D].rearrange("p (s c f) -> p s c f", s=SLOTS, c=CHUNK)
        fin_stage = work[:, 0:SLOTS * CW].rearrange("p (s n) -> p s n", s=SLOTS)
        hl = work[:, 0:SLOTS * CW].rearrange("p (s n) -> p s n", s=SLOTS)[0:D]

        ps_t = ps("ps_t", 1)
        ps_selt_f = ps("ps_selt", 1)
        ps_selt = ps_selt_f[:, :].bitcast(BF16)
        ps_win = ps_selt_f[0:D, 0:REACH]
        ps_pre = [ps("ps_pre0", 2), ps("ps_pre1", 2)]
        ps_agg = ps("ps_agg", 1)
        ps_deg = ps("ps_deg", 1)
        ps_fin = [ps_t, ps_agg, ps_deg]
        ps_sums = [ps_agg, ps_t]

        ld_idx = sem("ld_idx")
        ld_x = sem("ld_x")
        ld_w = sem("ld_w")
        const_made = sem("const_made")
        pool_step = sem("pool_step")
        dve_step = sem("dve_step")
        viol_ready = sem("viol_ready")
        viol_t = sem("viol_t")
        flag_ready = sem("flag_ready")
        var_ready = sem("var_ready")
        std_ready = sem("std_ready")
        h_ready = sem("h_ready")
        table_clear = sem("table_clear")
        np_h = sem("np_h")
        np_t = sem("np_t")
        np_tc = sem("np_tc")
        np_mm = sem("np_mm")
        np_c = sem("np_c")
        np_st = [sem(f"np_st{k}") for k in range(SLOTS)]
        ld_grp = [sem(f"ld_grp{q}") for q in range(RING)]
        ld_src = [sem(f"ld_src{q}") for q in range(RING)]
        gat = [sem(f"gat{q}") for q in range(RING)]
        sel_ready = sem("sel_ready")
        selb_ready = sem("selb_ready")
        selt_done = sem("selt_done")
        selt_copied = sem("selt_copied")
        hot_ready = sem("hot_ready")
        hist_done = sem("hist_done")
        pre_done = sem("pre_done")
        summed = sem("summed")
        hid_ready = sem("hid_ready")
        agg_done = sem("agg_done")
        added = sem("added")
        gen = [{n: sem(f"gen{L}_{n}") for n in ("zero_made", "zero_st", "ld", "dstf", "gat", "dstt", "eadot", "sel", "row", "comb", "combc",
                                                "scat", "free", "hot", "hist", "fold_ld", "fold_diag", "fold_t", "fold_c")}
               for L in range(2)]
        edges_done = sem("edges_done")
        hist_closed = sem("hist_closed")
        nu_ld = [sem(f"nu_ld{k}") for k in range(SLOTS)]
        nu_m = sem("nu_m")
        nu_mc = sem("nu_mc")
        nu_u = sem("nu_u")
        nu_uc = sem("nu_uc")
        nu_y = sem("nu_y")
        nu_x = sem("nu_x")
        deg_ready = sem("deg_ready")
        deg_root = sem("deg_root")
        st_h = sem("st_h")
        iota_made = sem("iota_made")
        split = sem("split")
        parts_ready = sem("parts_ready")
        hotlo_ready = sem("hotlo_ready")
        staged = sem("staged")
        code_ready = sem("code_ready")
        count_done = sem("count_done")
        count_copied = sem("count_copied")
        dense_done = sem("dense_done")
        reduced = sem("reduced")
        win_done = sem("win_done")
        ld_src1 = [sem(f"ld_src1_{q}") for q in range(RING)]
        gat1 = [sem(f"gat1_{q}") for q in range(RING)]
        sel1_ready = sem("sel1_ready")
        agg1_done = sem("agg1_done")
        table_added = sem("table_added")
        edges1_done = sem("edges1_done")
        in_ready = sem("in_ready")
        in_root = sem("in_root")
        fin_scaled = sem("fin_scaled")
        fin_t = sem("fin_t")
        fin_x = sem("fin_x")
        st_out = sem("st_out")

        def load_flag(eng, L):
            eng.wait_ge(flag_ready, 1)
            return eng.value_load(flag_i[0:1, L:L + 1], min_val=0, max_val=1)

        block = ctx.enter_context(nc.Block())

        @block.sync
        def _(sp):
            sp.dma_start(dst_i, dst_t).then_inc(ld_idx, 16)
            sp.dma_start(src_i, src_t).then_inc(ld_idx, 16)
            sp.dma_start(x[:], x_t).then_inc(ld_x, 16)
            sp.dma_start(w1ab[0:D, 0:H], mW1[0:D, :]).then_inc(ld_w, 16)
            sp.dma_start(w1ab[0:D, H:2 * H], mW1[D:2 * D, :]).then_inc(ld_w, 16)
            sp.dma_start(w1ab[D:D + 1, H:2 * H], mb1.rearrange("(a f) -> a f", a=1)).then_inc(ld_w, 16)
            for q in range(RING):
                sp.dma_start(rhs[WINDOW:WINDOW + De, q, :], mW1[2 * D:2 * D + De, :]).then_inc(ld_w, 16)
            sp.dma_start(w2[:], mW2).then_inc(ld_w, 16)
            sp.dma_start(u1a[:], uW1[0:D, :]).then_inc(ld_w, 16)
            sp.dma_start(u1b[:], uW1[D:2 * D, :]).then_inc(ld_w, 16)
            sp.dma_start(u2[:], uW2).then_inc(ld_w, 16)
            sp.dma_start(mb2_c[:], mb2.rearrange("(f a) -> f a", a=1)).then_inc(ld_w, 16)
            sp.dma_start(ub1_c[:], ub1.rearrange("(f a) -> f a", a=1)).then_inc(ld_w, 16)
            sp.dma_start(ub2_r[:], ub2.rearrange("(a f) -> a f", a=1)).then_inc(ld_w, 16)

            a_rows = table_a.rearrange("(t p) f -> p t f", p=P)
            b_rows = table_b.rearrange("(t p) f -> p t f", p=P)
            with sp.Fori(0, NCH) as i:
                for k in range(SLOTS):
                    c = i * SLOTS + k
                    sp.wait_ge(np_c, c + 2)
                    sp.dma_start(a_rows[:, bass.ds(c * CHUNK, CHUNK), :], abc[:, k, :, 0:H]).then_inc(np_st[k], 16)
                    sp.dma_start(b_rows[:, bass.ds(c * CHUNK, CHUNK), :], abc[:, k, :, H:2 * H]).then_inc(np_st[k], 16)
                    sp.dma_start(ht_dram[:, bass.ds(c * CW, CW)], htc[0:D, k, :]).then_inc(np_st[k], 16)
            for k in range(SLOTS):
                sp.wait_ge(np_st[k], 48 * NCH + 48)

            def group_loads():
                def operands(g, q):
                    base = sp.value_load(bases[0:1, bass.ds(g + 1, 1)], min_val=0, max_val=n_nodes)
                    sp.wait_ge(pre_done, g + 1)
                    sp.dma_start(lhs[WINDOW:WINDOW + De, q, :], ea_t[:, bass.ds(g * GROUP, GROUP)]).then_inc(ld_grp[q], 16)
                    sp.dma_start(rhs[0:WINDOW, q, :], table_b[bass.ds(base, WINDOW), :]).then_inc(ld_grp[q], 16)

                with sp.Fori(0, NI) as i:
                    for q in range(RING):
                        g = i * RING + q
                        operands(g, q)
                        sp.wait_ge(summed, g + 1)
                        sp.dma_start(idx[:, q, :], src_t[:, bass.ds(g * TILES, TILES)]).then_inc(ld_src[q], 16)
                operands(N0, 0)

            def general_loads(L):
                s, width = gen[L], (H + 1, D)[L]
                zero = hid[:, 0, 0:2, :].rearrange("p j f -> p (j f)")[:, 0:width]
                rows = sums[L].rearrange("(t p) f -> p t f", p=P)
                sp.wait_ge(s["zero_made"], 1)
                with sp.Fori(0, NT + 1) as t:
                    sp.dma_start(rows[:, bass.ds(t, 1), :], zero.unsqueeze(1)).then_inc(s["zero_st"], 16)
                with sp.Fori(0, NG) as g:
                    sp.wait_ge(s["free"], g * TILES + 1)
                    sp.nop(nofuse=True)
                    sp.dma_start(idx[:, 0, :], src_t[:, bass.ds(g * TILES, TILES)]).then_inc(s["ld"], 16)
                    sp.dma_start(idx[:, 1, :], dst_t[:, bass.ds(g * TILES, TILES)]).then_inc(s["ld"], 16)
                    if L == 0:
                        sp.dma_start(lhs[WINDOW:WINDOW + De, 0, :], ea_t[:, bass.ds(g * GROUP, GROUP)]).then_inc(s["ld"], 16)
                sp.wait_ge(s["free"], NG * TILES + 1)
                with sp.Fori(0, NT) as t:
                    sp.wait_ge(s["fold_c"], t + 1)
                    sp.dma_start(gathered[:, 0, 0:2, :].rearrange("p j f -> p (j f)")[:, 0:width].unsqueeze(1),
                                 rows[:, bass.ds(t, 1), :]).then_inc(s["fold_ld"], 16)

            general = load_flag(sp, 0)
            with sp.If(general > 0):
                general_loads(0)
            with sp.Else():
                group_loads()

            sp.wait_ge(edges_done, 1)
            with sp.Fori(0, NCH) as i:
                for k in range(SLOTS):
                    c = i * SLOTS + k
                    sp.wait_ge(nu_u, c + 1)
                    sp.dma_start(hl[:, k, :], ht_dram[:, bass.ds(c * CW, CW)]).then_inc(nu_ld[k], 16)
            sp.wait_ge(h_ready, 2)
            sp.dma_start(table_h.rearrange("(t p) f -> p t f", p=P), h2).then_inc(st_h, 16)

            def source_loads():
                with sp.Fori(0, NI1) as i:
                    for q in range(RING):
                        g = i * RING + q
                        sp.wait_ge(agg1_done, g + 1)
                        sp.dma_start(idx[:, q, :], src_t[:, bass.ds(g * TILES, TILES)]).then_inc(ld_src1[q], 16)

            sp.wait_ge(st_h, 16)
            general = load_flag(sp, 1)
            with sp.If(general > 0):
                general_loads(1)
            with sp.Else():
                source_loads()

            sp.wait_ge(fin_x, NCH * SLOTS + SLOTS)
            sp.dma_start(out_t, x[:]).then_inc(st_out, 16)
            sp.wait_ge(st_out, 16)

        @block.gpsimd
        def _(pool):
            pool.memset(ones[:], 1.0).then_inc(const_made, 1)
            pool.memset(ident[:], 0.0).then_inc(pool_step, 1)
            pool.wait_ge(pool_step, 1)
            pool.affine_select(out=ident[:], in_=ident[:], compare_op=ALU.not_equal, fill=1.0, base=0,
                               pattern=[[-1, P]], channel_multiplier=1).then_inc(const_made, 1)
            pool.iota(iota_i[:], pattern=[[1, P]], base=0, channel_multiplier=0).then_inc(const_made, 1)
            pool.memset(eps_c[:], EPS).then_inc(const_made, 1)
            pool.wait_ge(h_ready, 1)
            with pool.Fori(0, NCH) as i:
                for k in range(SLOTS):
                    c = i * SLOTS + k
                    pool.wait_ge(np_t, c + 1)
                    pool.tensor_copy(h_stage[:, k, :, :], h[:, bass.ds(c * CHUNK, CHUNK), :]).then_inc(np_h, 1)
            for k in range(SLOTS):
                pool.wait_ge(np_st[k], 48 * NCH + 48)
            pool.wait_ge(flag_ready, 1)
            pool.memset(table[:], 0.0).then_inc(table_clear, 1)

            def gathers(trips, rows, ring, loaded, done, freed):
                with pool.Fori(0, trips) as i:
                    for q in range(RING):
                        pool.wait_ge(loaded[q], 16 * i + 16)
                        pool.wait_ge(freed, i * RING + q + 1)
                        pool.nop(nofuse=True)
                        for j in range(TILES):
                            pool.indirect_dma_start(ring[:, q, j, :], None, rows,
                                                    bass.IndirectOffsetOnAxis(ap=idx[:, q, j:j + 1], axis=0)
                                                    ).then_inc(done[q], 16)

            def general_gathers(L):
                s, width = gen[L], (H + 1, D)[L]
                pool.wait_ge(s["zero_st"], 16 * (NT + 1))
                with pool.Fori(0, NG) as g:
                    pool.wait_ge(s["ld"], (48, 32)[L] * g + (48, 32)[L])
                    pool.nop(nofuse=True)
                    for j in range(TILES):
                        if L == 0:
                            pool.indirect_dma_start(gathered[:, 0, 0, :], None, table_a,
                                                    bass.IndirectOffsetOnAxis(ap=idx[:, 0, j:j + 1], axis=0)).then_inc(s["gat"], 16)
                            pool.indirect_dma_start(gathered[:, 0, 1, :], None, table_b,
                                                    bass.IndirectOffsetOnAxis(ap=idx[:, 1, j:j + 1], axis=0)).then_inc(s["gat"], 16)
                        else:
                            pool.indirect_dma_start(gathered_h[:, 0, 0, :], None, table_h,
                                                    bass.IndirectOffsetOnAxis(ap=idx[:, 0, j:j + 1], axis=0)).then_inc(s["gat"], 16)
                        pool.wait_ge(s["combc"], g * TILES + j + 1)
                        pool.nop(nofuse=True)
                        pool.indirect_dma_start(sums[L], bass.IndirectOffsetOnAxis(ap=idx[:, 2, 0:1], axis=0),
                                                hid[:, 1, 0:2, :].rearrange("p j f -> p (j f)")[:, 0:width], None,
                                                compute_op=ALU.add).then_inc(s["scat"], 16)
                        pool.wait_ge(s["scat"], g * (16 * TILES) + 16 * j + 16)
                        pool.sem_inc(s["free"], 1)

            general = load_flag(pool, 0)
            with pool.If(general > 0):
                general_gathers(0)
            with pool.Else():
                gathers(NI, table_a, gathered, ld_src, gat, summed)
            pool.wait_ge(edges_done, 1)
            pool.iota(iota_ci, pattern=[[1, HI * SPAN]], base=0, channel_multiplier=0).then_inc(iota_made, 1)
            pool.wait_ge(st_h, 16)
            general = load_flag(pool, 1)
            with pool.If(general > 0):
                general_gathers(1)
            with pool.Else():
                gathers(NI1, table_h, ring1, ld_src1, gat1, agg1_done)

        @block.scalar
        def _(act):
            def std(n):
                act.wait_ge(var_ready, n + 1)
                act.activation(rstd[:], mean[:], ACT.Sqrt, bias=eps_c[:, 0:1], scale=1.0 / D).then_inc(std_ready, 1)

            act.wait_ge(const_made, 15)
            std(0)
            act.wait_ge(h_ready, 1)
            with act.Fori(0, NCH) as i:
                for k in range(SLOTS):
                    c = i * SLOTS + k
                    act.wait_ge(np_t, c + SLOTS + 1)
                    act.wait_ge(np_st[k], 48 * i + 48)
                    act.copy(htc[0:D, k, :], ps_t[0:D, 0:CW]).then_inc(np_tc, 1)

            def selt_copy(g, q):
                act.wait_ge(selt_done, g + 1)
                act.wait_ge(pre_done, g + 1)
                act.copy(lhs[0:WINDOW, q, :], ps_selt[0:WINDOW, 0:GROUP]).then_inc(selt_copied, 1)

            def sel_copy(g, slot):
                act.wait_ge(sel_ready, g + 1)
                act.wait_ge(agg_done, g + 3)
                act.copy(sel_b[:, slot % 2, :, :], sel[:, slot, :, :]).then_inc(selb_ready, 1)

            def fast_hidden():
                sel_copy(0, 0)
                selt_copy(0, 0)
                with act.Fori(0, NI) as i:
                    for q in range(RING):
                        g = i * RING + q
                        sel_copy(g + 1, (q + 1) % RING)
                        selt_copy(g + 1, (q + 1) % RING)
                        act.wait_ge(summed, g + RING + 1)
                        act.activation(hid[:, q % 2, :, :], hid[:, q % 2, :, :], ACT.Relu).then_inc(hid_ready, 1)

            general = load_flag(act, 0)
            with act.If(general > 0):
                act.nop()
            with act.Else():
                fast_hidden()

            act.wait_ge(edges_done, 1)
            with act.Fori(0, NCH) as i:
                for k in range(SLOTS):
                    c = i * SLOTS + k
                    act.wait_ge(nu_u, c + SLOTS + 1)
                    act.wait_ge(nu_y, c + 1)
                    act.activation(utc, ps_pre[1][:, 0:CW], ACT.Relu, bias=ub1_c[:, 0:1]).then_inc(nu_uc, 1)
            act.wait_ge(deg_ready, 1)
            act.activation(inv_out[:], inv_out[:], ACT.Sqrt).then_inc(deg_root, 1)
            std(1)
            act.wait_ge(in_ready, 1)
            act.activation(table[D:P, 0, :], table[D:P, 0, :], ACT.Sqrt).then_inc(in_root, 1)

            def copy_counts():
                act.wait_ge(st_h, 16)
                act.wait_ge(parts_ready, 1)
                with act.Fori(0, NI1) as i:
                    for hf in range(2):
                        h = 2 * i + hf
                        act.wait_ge(dense_done, h + 1)
                        for tile in range(HALF):
                            act.wait_ge(count_done, h * HALF + tile + CODES + 1)
                            to = counts[:, hf, :, tile * SPAN:(tile + 1) * SPAN].rearrange("p (a b) n -> p a b n", a=2)
                            act.copy(to, ps_pre[tile % 2][:, :].rearrange("p (a x) -> p a x", a=2)[:, :, 0:HI // 2 * SPAN]
                                     .rearrange("p a (b n) -> p a b n", n=SPAN)).then_inc(count_copied, 1)

            general = load_flag(act, 1)
            with act.If(general > 0):
                act.nop()
            with act.Else():
                copy_counts()
            act.wait_ge(edges1_done, 1)
            with act.Fori(0, NCH) as i:
                for k in range(SLOTS):
                    c = i * SLOTS + k
                    act.wait_ge(fin_t, c + 1)
                    act.copy(fin_stage[:, k, :], table[:, 0, bass.ds(c * CW, CW)]).then_inc(fin_scaled, 1)

        @block.vector
        def _(dve):
            steps = [0]

            def step(ins):
                steps[0] += 1
                ins.then_inc(dve_step, 1)
                dve.wait_ge(dve_step, steps[0])

            def across(column, n):
                return column.unsqueeze(2).broadcast_to([P, NT, n])

            def normalise(n, scale, h, square):
                step(dve.tensor_reduce(mean[:], x[:], AX.X, ALU.add))
                step(dve.tensor_scalar(mean[:], mean[:], 1.0 / D, None, ALU.mult))
                step(dve.tensor_tensor(h, x[:], across(mean[:], D), ALU.subtract))
                step(dve.tensor_tensor(square, h, h, ALU.mult))
                step(dve.tensor_reduce(mean[:], square, AX.X, ALU.add))
                dve.sem_inc(var_ready, 1)
                dve.wait_ge(std_ready, n + 1)
                step(dve.reciprocal(rstd[:], rstd[:]))
                if scale is not None:
                    step(dve.tensor_tensor(rstd[:], rstd[:], scale[:], ALU.mult))
                dve.scalar_tensor_tensor(h, h, 0.0, across(rstd[:], D), ALU.max, ALU.mult).then_inc(h_ready, 1)

            dve.memset(w1ab[D:D + 1, 0:H], 0.0).then_inc(const_made, 1)
            dve.memset(htc[D:D + 1, :, :], 1.0).then_inc(const_made, 1)
            dve.memset(zero_r[:], 0.0).then_inc(const_made, 1)
            dve.memset(node_of[:], 0.0).then_inc(const_made, 1)
            step(dve.memset(hid_flat[0:1, :], 0.0))
            step(dve.memset(tile_row[0:1, SPAN:V], -1.0))
            dve.memset(tile_row.rearrange("p (j x) -> p j x", x=V + SPAN)[:, 1:HALF, 0:SPAN], 1.0).then_inc(const_made, 1)
            for k in range(1, SPAN):
                dve.memset(mod_row.rearrange("p (j k) -> p j k", k=SPAN)[:, :, k:k + 1], float(k)).then_inc(const_made, 1)
            dve.wait_ge(const_made, 15)
            dve.tensor_copy(iota_f[:], iota_i[:])
            dve.tensor_copy(iota_b[:], iota_i[:])
            dve.tensor_copy(ident_b[:], ident[:])
            dve.tensor_copy(ones_b[:], ones[:])
            dve.memset(dst_rel[:, T:T + TILES], 0)
            dve.memset(src_hi[:, T:T + TILES], 0)
            dve.memset(src_lo[:, T:T + TILES], 0)
            dve.memset(bases[0:1, 0:1], 0)
            dve.memset(bases[0:1, NG + 1:NG + 2], 0)
            dve.memset(small[:], 0.0)
            dve.memset(code[:, T - T1:T - T1 + TILES], 0.0)
            dve.wait_ge(ld_idx, 32)
            dve.tensor_copy(bases[0:1, 1:NG + 1], dst_i[0:1, 0:T:TILES])
            dve.tensor_copy(dst_f, dst_i)
            step(dve.tensor_scalar(shifted, src_i, 7, None, ALU.arith_shift_right))
            step(dve.tensor_copy(src_hi[:, 0:T], shifted))
            step(dve.tensor_scalar(shifted, src_i, P - 1, None, ALU.bitwise_and))
            step(dve.tensor_copy(src_lo[:, 0:T], shifted))
            dve.sem_inc(viol_ready, 1)
            dve.wait_ge(viol_t, 1)
            dve.tensor_copy(node_of[:, 1:NH + 1], ps_deg[0:V, 0:NH])
            for c in range(0, T - T1, 512):
                n = min(512, T - T1 - c)
                dve.tensor_tensor(rel_tile[:, c:c + n], dst_f[:, T1 + c:T1 + c + n],
                                  ps_pre[c // 1024][:, c % 1024:c % 1024 + n], ALU.subtract)
            by_half = lambda a: a.rearrange("p (h j) -> p h j", j=HALF)
            step(dve.tensor_tensor(by_half(rel_half), by_half(dst_f[:, T1:T]),
                                   ps_agg[:, P:P + NH].unsqueeze(2).broadcast_to([P, NH, HALF]), ALU.subtract))
            for k, (rel, limit) in enumerate(((rel_tile, SPAN), (rel_half, REACH))):
                o = 8 + 3 * k
                step(dve.tensor_reduce(small[:, o:o + 1], rel, AX.X, ALU.max))
                step(dve.tensor_reduce(small[:, o + 1:o + 2], rel, AX.X, ALU.min))
                step(dve.tensor_scalar(small[:, o:o + 1], small[:, o:o + 1], float(1 - limit), None, ALU.add))
                step(dve.scalar_tensor_tensor(small[:, o + 2:o + 3], small[:, o + 1:o + 2], -1.0, small[:, o:o + 1], ALU.mult, ALU.max))
            step(dve.tensor_tensor(small[:, 14:15], small[:, 10:11], small[:, 13:14], ALU.max))
            step(dve.tensor_scalar(rel_tile, rel_tile, -1.0, float(SPAN), ALU.max, ALU.min))
            dve.scalar_tensor_tensor(code[:, 0:T - T1], src_hi[:, T1:T], float(SPAN), rel_tile, ALU.mult, ALU.add)
            rel3 = dst_f.rearrange("p (g j) -> p g j", j=TILES)
            step(dve.tensor_tensor(rel3, rel3, ps_t[:, 0:NG].unsqueeze(2).broadcast_to([P, NG, TILES]), ALU.subtract))
            dve.tensor_copy(dst_rel[:, 0:T], dst_f)
            step(dve.tensor_reduce(small[:, 0:1], dst_f, AX.X, ALU.max))
            step(dve.tensor_reduce(small[:, 1:2], dst_f, AX.X, ALU.min))
            step(dve.tensor_scalar(small[:, 0:1], small[:, 0:1], float(1 - WINDOW), None, ALU.add))
            step(dve.scalar_tensor_tensor(small[:, 2:3], small[:, 1:2], -1.0, small[:, 0:1], ALU.mult, ALU.max))
            step(dve.tensor_tensor(small[:, 15:16], small[:, 14:15], small[:, 2:3], ALU.max))
            dve.sem_inc(viol_ready, 1)
            dve.wait_ge(viol_t, 2)
            step(dve.tensor_reduce(small[0:1, 8:10], ps_t[0:1, 0:2 * P].rearrange("p (a n) -> p a n", a=2), AX.X, ALU.max))
            dve.tensor_scalar(flag_i[:], small[0:1, 8:10], 0.0, None, ALU.is_gt).then_inc(flag_ready, 1)

            dve.wait_ge(ld_x, 16)
            normalise(0, None, h, square)
            dve.wait_ge(h_ready, 1)
            with dve.Fori(0, NCH) as i:
                for k in range(SLOTS):
                    c = i * SLOTS + k
                    dve.wait_ge(np_mm, c + 1)
                    dve.wait_ge(np_st[k], 48 * i + 48)
                    dve.tensor_copy(abc[:, k, :, :], ps_pre[0][:, 0:CHUNK * 2 * H].rearrange("p (c f) -> p c f", c=CHUNK)).then_inc(np_c, 1)

            iota_w = iota_b[:, 0:WINDOW].unsqueeze(1).broadcast_to([P, TILES, WINDOW])

            def make_sel(col, slot, ready):
                rel = dst_rel[:, bass.ds(col, TILES)].unsqueeze(2).broadcast_to([P, TILES, WINDOW])
                dve.tensor_tensor(sel[:, slot, :, :], rel, iota_w, ALU.is_equal).then_inc(ready, 1)

            def make_hot(col, slot, ready):
                hi = src_hi[:, bass.ds(col, TILES)].unsqueeze(2)
                lo = src_lo[:, bass.ds(col, TILES)].unsqueeze(2)
                dve.tensor_tensor(hot_hi[:, slot, :, :], hi.broadcast_to([P, TILES, NT]),
                                  iota_b[:, 0:NT].unsqueeze(1).broadcast_to([P, TILES, NT]), ALU.is_equal).then_inc(ready, 1)
                dve.tensor_tensor(hot_lo[:, slot, :, :], lo.broadcast_to([P, TILES, P]),
                                  iota_b[:, :].unsqueeze(1).broadcast_to([P, TILES, P]), ALU.is_equal).then_inc(ready, 1)

            def add_window(base, slot, rows, halves, done, n):
                dve.wait_ge(done, n)
                spot = table[0:rows, 0:halves, bass.ds(base, WINDOW)]
                new = ps_sums[slot][0:rows, 0:halves * WINDOW].rearrange("p (a n) -> p a n", a=halves)
                dve.tensor_tensor(spot, spot, new, ALU.add).then_inc(done, 1)

            def fast_layer0():
                dve.wait_ge(table_clear, 1)
                dve.wait_ge(agg_done, 1)
                make_sel(0, 0, sel_ready)
                dve.wait_ge(hist_done, 1)
                make_hot(0, 0, hot_ready)
                with dve.Fori(0, NI) as i:
                    for q in range(RING):
                        g = i * RING + q
                        base = dve.value_load(bases[0:1, bass.ds(g, 1)], min_val=0, max_val=n_nodes)
                        dve.wait_ge(agg_done, g + 2)
                        make_sel((g + 1) * TILES, (q + 1) % RING, sel_ready)
                        dve.wait_ge(hist_done, g + 2)
                        make_hot((g + 1) * TILES, (q + 1) % 2, hot_ready)
                        dve.wait_ge(pre_done, g + RING + 1)
                        dve.wait_ge(gat[q], 16 * TILES * i + 16 * TILES)
                        dve.wait_ge(agg_done, g + 3)
                        for half in range(2):
                            t0 = half * TILES // 2
                            ins = dve.tensor_tensor(
                                hid[:, q % 2, t0:t0 + TILES // 2, :], gathered[:, q, t0:t0 + TILES // 2, :],
                                ps_pre[q % 2][:, 512 * half:512 * half + 512].rearrange("p (j f) -> p j f", f=H), ALU.add)
                        ins.then_inc(summed, 1)
                        dve.wait_ge(agg_done, g + 4)
                        add_window(base, (q + 1) % 2, P, 2, added, g + 2)
                base = dve.value_load(bases[0:1, N0:N0 + 1], min_val=0, max_val=n_nodes)
                dve.wait_ge(agg_done, N0 + 4)
                add_window(base, (N0 + 1) % 2, P, 2, added, N0 + 2)
                dve.wait_ge(added, N0 + 3)

            def general_layer(L):
                s, width = gen[L], (H + 1, D)[L]
                if L == 0:
                    dve.wait_ge(table_clear, 1)
                dve.memset(hid[:, 0, 0:2, :], 0.0).then_inc(s["zero_made"], 1)
                dve.wait_ge(s["zero_st"], 16 * (NT + 1))
                val = hid[:, 0, 0:2, :].rearrange("p j f -> p (j f)")
                out_rows = hid[:, 1, 0:2, :].rearrange("p j f -> p (j f)")[:, 0:width]
                dstf, eq, low = small[:, 4:5], gathered[:, 1, 0, :], gathered[:, 1, 1, :]
                n = [0]

                def link(ins, g, sem_name="row", per=0):
                    n[0] += 1
                    ins.then_inc(s[sem_name], 1)
                    dve.wait_ge(s[sem_name], g * per + n[0])

                per_tile = 6 if L == 0 else 4
                dve.memset(val[:, H:H + 1], 1.0).then_inc(s["row"], 1)
                dve.wait_ge(s["row"], 1)
                n[0] = 1
                with dve.Fori(0, NG) as g:
                    dve.wait_ge(s["ld"], (48, 32)[L] * g + (48, 32)[L])
                    if L == 0:
                        dve.wait_ge(s["hist"], g + 1)
                        make_hot(g * TILES, 0, s["hot"])
                    for j in range(TILES):
                        dve.wait_ge(s["dstt"], g * TILES + j + 1)
                        dve.wait_ge(s["free"], g * TILES + j + 1)
                        dve.tensor_copy(dstf, idx[:, 1, j:j + 1]).then_inc(s["dstf"], 1)
                        dve.wait_ge(s["dstf"], g * TILES + j + 1)
                        dve.wait_ge(s["dstt"], g * TILES + j + 2)
                        link(dve.tensor_scalar(eq, ps_t[:, 0:P], dstf, None, ALU.is_equal), g, "row", per_tile * TILES)
                        link(dve.scalar_tensor_tensor(low, iota_f[:, :], small[:, 5:6], eq, ALU.is_lt, ALU.mult), g, "row", per_tile * TILES)
                        link(dve.tensor_reduce(small[:, 6:7], low, AX.X, ALU.max), g, "row", per_tile * TILES)
                        link(dve.scalar_tensor_tensor(small[:, 7:8], small[:, 5:6], float(NP), dstf, ALU.add, ALU.subtract), g, "row", per_tile * TILES)
                        dve.scalar_tensor_tensor(idx[:, 2, 0:1], small[:, 7:8], small[:, 6:7], dstf, ALU.mult, ALU.add).then_inc(s["sel"], 1)
                        dve.wait_ge(s["gat"], ((32 * TILES) if L == 0 else 16 * TILES) * g + (32 if L == 0 else 16) * (j + 1))
                        if L == 0:
                            dve.wait_ge(s["eadot"], g * TILES + j + 1)
                            link(dve.tensor_tensor(gathered[:, 0, 0, :], gathered[:, 0, 0, :], gathered[:, 0, 1, :], ALU.add), g, "row", per_tile * TILES)
                            link(dve.tensor_tensor(gathered[:, 0, 0, :], gathered[:, 0, 0, :], ps_pre[0][:, 0:H], ALU.add), g, "row", per_tile * TILES)
                            dve.tensor_scalar(val[:, 0:H], gathered[:, 0, 0, :], 0.0, None, ALU.max).then_inc(s["sel"], 1)
                        dve.wait_ge(s["comb"], g * TILES + j + 1)
                        dve.tensor_copy(out_rows, ps_agg[:, 0:width]).then_inc(s["combc"], 1)
                with dve.Fori(0, NT) as t:
                    dve.wait_ge(s["fold_ld"], 16 * t + 16)
                    if L == 0:
                        dve.tensor_scalar(eq, ident[:, :], gathered[:, 0, 1, 0:1], None, ALU.mult).then_inc(s["fold_diag"], 1)
                    dve.wait_ge(s["fold_t"], t + 1)
                    if L == 0:
                        dve.tensor_copy(table[:, :, bass.ds(t * P, P)],
                                        ps_t[:, 0:2 * P].rearrange("p (a n) -> p a n", a=2)).then_inc(s["fold_c"], 1)
                    else:
                        dve.tensor_copy(table[0:D, 0, bass.ds(t * P, P)], ps_t[0:D, 0:P]).then_inc(s["fold_c"], 1)
                dve.wait_ge(s["fold_c"], NT + 1)

            dve.wait_ge(flag_ready, 1)
            dve.wait_ge(viol_t, 3)
            dve.tensor_copy(small[:, 5:6], ps_agg[:, 0:1]).then_inc(viol_ready, 1)
            dve.wait_ge(viol_ready, 3)
            general = load_flag(dve, 0)
            with dve.If(general > 0):
                general_layer(0)
            with dve.Else():
                fast_layer0()
            dve.sem_inc(edges_done, 1)

            with dve.Fori(0, NCH) as i:
                for k in range(SLOTS):
                    c = i * SLOTS + k
                    dve.wait_ge(nu_m, c + 1)
                    dve.wait_ge(nu_u, c + SLOTS)
                    dve.scalar_tensor_tensor(mtc, table[0:D, 1, bass.ds(c * CW, CW)], mb2_c[:, 0:1], ps_pre[0][0:D, 0:CW],
                                             ALU.mult, ALU.add).then_inc(nu_mc, 1)
                    dve.wait_ge(nu_y, c + 2)
                    rows = x[:, bass.ds(c * CHUNK, CHUNK), :]
                    dve.tensor_tensor(rows, rows, ps_agg[:, 0:CHUNK * D].rearrange("p (c f) -> p c f", c=CHUNK),
                                      ALU.add).then_inc(nu_x, 1)
            dve.wait_ge(nu_x, NCH * SLOTS + 1)
            dve.wait_ge(hist_closed, 1)
            dve.tensor_scalar(inv_out[:], ps_deg[:, 0:NT], 1.0, None, ALU.max).then_inc(deg_ready, 1)
            dve.tensor_scalar(table[D:P, 0, :], table[D:P, 1, :], 1.0, None, ALU.max).then_inc(in_ready, 1)
            dve.wait_ge(in_ready, 1)
            dve.memset(table[0:D, 0, :], 0.0)
            dve.wait_ge(deg_root, 1)
            step(dve.reciprocal(inv_out[:], inv_out[:]))
            normalise(1, inv_out, h2, square2)

            def split_rows():
                rows, rest = h2[:, 0:HI, :], square2[:, 0:HI, :]

                def then(ins, n):
                    ins.then_inc(split, 1)
                    dve.wait_ge(split, n)

                dve.wait_ge(iota_made, 1)
                then(dve.tensor_copy(iota_c, iota_ci), 1)
                dve.wait_ge(h_ready, 2)
                then(dve.tensor_copy(parts[:, :, 0, :], rows), 2)
                then(dve.tensor_tensor(rest, rows, parts[:, :, 0, :], ALU.subtract), 3)
                then(dve.tensor_copy(parts[:, :, 1, :], rest), 4)
                then(dve.tensor_tensor(rest, rest, parts[:, :, 1, :], ALU.subtract), 5)
                then(dve.tensor_copy(parts[:, :, 2, :], rest), 6)
                dve.wait_ge(st_h, 16)
                then(dve.memset(counts[:, 1, :, :], 0.0), 7)
                dve.sem_inc(parts_ready, 1)

            def fast_layer1():
                def next_group(d, g, slot):
                    lo = src_lo[:, bass.ds(T1 + d * TILES, TILES)].unsqueeze(2)
                    dve.tensor_tensor(hot_lo[:, slot, :, :], lo.broadcast_to([P, TILES, P]),
                                      iota_b[:, :].unsqueeze(1).broadcast_to([P, TILES, P]), ALU.is_equal).then_inc(hotlo_ready, 1)
                    dve.tensor_copy(code_s[:, slot, :], code[:, bass.ds(d * TILES, TILES)]).then_inc(staged, 1)
                    make_sel(g * TILES, slot, sel1_ready)

                def add(base, sums, width, n):
                    dve.wait_ge(table_added, n)
                    spot = table[0:D, 0, bass.ds(base, width)]
                    dve.tensor_tensor(spot, spot, sums, ALU.add).then_inc(table_added, 1)

                def place_rows(h):
                    dve.tensor_tensor(place, iota_f[0:V, 0:REACH], node_of[:, bass.ds(h, 1)].broadcast_to([V, REACH]), ALU.is_equal)

                def sum_parts(h):
                    dve.wait_ge(dense_done, h + 2)
                    dve.tensor_reduce(summed_rows, ps_t[0:V, 0:3 * D].rearrange("p (a d) -> p d a", a=3), AX.X,
                                      ALU.add).then_inc(reduced, 1)

                dve.wait_ge(agg1_done, RING)
                dve.wait_ge(count_done, CODES)
                next_group(0, 0, 0)
                with dve.Fori(0, NI1) as i:
                    for hf in range(2):
                        h = 2 * i + hf
                        base = [dve.value_load(bases[0:1, bass.ds(n, 1)], min_val=0, max_val=n_nodes)
                                for n in (2 * h + 1, 2 * h + 2, G1 + 2 * h - 3)]
                        for tile in range(HALF):
                            dve.wait_ge(count_done, h * HALF + tile + 1)
                            dve.wait_ge(staged, 2 * h + tile // TILES + 1)
                            dve.tensor_scalar(hot_code[:, tile % CODES, :], iota_c,
                                              code_s[:, tile // TILES, tile % TILES:tile % TILES + 1], None,
                                              ALU.is_equal).then_inc(code_ready, 1)
                            if tile % TILES == CODES:
                                k = tile // TILES
                                dve.wait_ge(agg1_done, 2 * h + k + RING + 1)
                                add(base[k], ps_agg[0:D, 0:WINDOW], WINDOW, 3 * h + 2 * k + 1)
                                next_group(2 * h + k + 1, 2 * h + k + 1, 1 - k)
                            if tile == CODES + 2:
                                dve.wait_ge(win_done, h + 1)
                                add(base[2], ps_win, REACH, 3 * h + 2)
                                place_rows(h)
                        sum_parts(h)
                base = [dve.value_load(bases[0:1, G1 + 2 * n + 1:G1 + 2 * n + 2], min_val=0, max_val=n_nodes)
                        for n in (NH - 2, NH - 1)]
                dve.wait_ge(win_done, NH + 1)
                add(base[0], ps_win, REACH, 3 * NH + 1)
                place_rows(NH)
                sum_parts(NH)
                dve.wait_ge(win_done, NH + 2)
                add(base[1], ps_win, REACH, 3 * NH + 2)
                dve.wait_ge(table_added, 3 * NH + 3)

            general = load_flag(dve, 1)
            with dve.If(general > 0):
                general_layer(1)
            with dve.Else():
                split_rows()
                fast_layer1()

            dve.wait_ge(in_root, 1)
            step(dve.reciprocal(table[D:P, 0, :], table[D:P, 0, :]))
            dve.sem_inc(edges1_done, 1)
            with dve.Fori(0, NCH) as i:
                for k in range(SLOTS):
                    c = i * SLOTS + k
                    dve.wait_ge(fin_t, c + SLOTS + 1)
                    for t in range(CHUNK):
                        row = x[:, bass.ds(c * CHUNK + t, 1), :].rearrange("p a d -> p (a d)")
                        ins = dve.scalar_tensor_tensor(row, ps_fin[k][:, t * P:t * P + D], ps_fin[k][:, t * P + D:t * P + D + 1],
                                                       row, ALU.mult, ALU.add)
                    ins.then_inc(fin_x, 1)

        @block.tensor
        def _(pe):
            pe.wait_ge(const_made, 15)
            pe.sem_inc(pre_done, RING)
            pe.sem_inc(summed, RING)
            pe.sem_inc(agg_done, RING - 1)
            pe.sem_inc(hist_done, 2)
            pe.sem_inc(added, 2)
            pe.sem_inc(agg1_done, RING)
            pe.sem_inc(table_added, 1)
            pe.sem_inc(count_done, CODES)
            pe.sem_inc(count_copied, 2)
            pe.sem_inc(dense_done, 1)
            pe.sem_inc(nu_u, SLOTS)
            pe.sem_inc(np_t, SLOTS)
            pe.sem_inc(fin_t, SLOTS)
            pe.sem_inc(nu_y, 1)
            pe.sem_inc(fin_x, SLOTS)
            pe.sem_inc(np_tc, 1)
            pe.sem_inc(np_c, 1)
            pe.sem_inc(selt_copied, 1)
            pe.sem_inc(nu_mc, 1)
            pe.sem_inc(nu_uc, 1)
            pe.sem_inc(nu_x, 1)
            for k in range(SLOTS):
                pe.sem_inc(np_st[k], 48)
            for L in range(2):
                pe.sem_inc(gen[L]["dstt"], 1)
                pe.sem_inc(gen[L]["hist"], 1)
                pe.sem_inc(gen[L]["free"], 1)
                pe.sem_inc(gen[L]["fold_c"], 1)
            pe.wait_ge(viol_ready, 1)
            pe.matmul(ps_t[:, 0:NG], ones[0:1, :], dst_f[0:1, 0:T:TILES], start=True, stop=True)
            pe.matmul(ps_agg[:, P:P + NH], ones[0:1, :], dst_f[0:1, T1:T:HALF], start=True, stop=True)
            for c in range(0, T - T1, 512):
                n = min(512, T - T1 - c)
                pe.matmul(ps_pre[c // 1024][:, c % 1024:c % 1024 + n], ones[0:1, :], dst_f[0:1, T1 + c:T1 + c + n],
                          start=True, stop=True)
            for j in range(HALF):
                pe.matmul(ps_deg[0:V, 0:NH], tile_row[0:1, j * V:(j + 1) * V], dst_f[0:1, T1 + j:T:HALF],
                          start=(j == 0), stop=False)
            pe.matmul(ps_deg[0:V, 0:NH], mod_row, ones[0:1, 0:1].broadcast_to([1, NH]), start=False, stop=True).then_inc(viol_t, 1)
            pe.wait_ge(viol_ready, 2)
            pe.matmul(ps_t[0:1, 0:P], small[:, 2:3], ident[:, :], start=True, stop=True)
            pe.matmul(ps_t[0:1, P:2 * P], small[:, 15:16], ident[:, :], start=True, stop=True).then_inc(viol_t, 1)
            pe.matmul(ps_agg[:, 0:1], iota_f[0:1, :], ones[0:1, 0:1], start=True, stop=True).then_inc(viol_t, 1)

            pe.wait_ge(flag_ready, 1)
            pe.wait_ge(h_ready, 1)
            pe.wait_ge(ld_w, 16 * (10 + RING))
            with pe.Fori(0, NCH) as i:
                for k in range(SLOTS):
                    c = i * SLOTS + k
                    pe.wait_ge(np_h, c + 1)
                    pe.wait_ge(np_tc, c + 1)
                    pe.nop(nofuse=True)
                    for t in range(CHUNK):
                        ins = pe.transpose(ps_t[0:D, t * P:(t + 1) * P], h_stage[:, k, t, :], ident[:, :])
                    ins.then_inc(np_t, 1)
                    pe.wait_ge(np_tc, c + 2)
                    pe.wait_ge(np_c, c + 1)
                    for t in range(CHUNK):
                        ins = pe.matmul(ps_pre[0][:, t * 2 * H:(t + 1) * 2 * H], htc[:, k, t * P:(t + 1) * P], w1ab[:, :],
                                        start=True, stop=True)
                    ins.then_inc(np_mm, 1)

            def open_hist():
                pe.matmul(ps_deg[:, 0:NT], ones[0:1, :], zero_r[:, 0:NT], start=True, stop=False, skip_group_check=True)

            def hist(slot, done):
                for j in range(TILES):
                    ins = pe.matmul(ps_deg[:, 0:NT], hot_lo[:, slot, j, :], hot_hi[:, slot, j, :],
                                    start=False, stop=False, skip_group_check=True)
                ins.then_inc(done, 1)

            def sel_transposed(g, slot):
                pe.wait_ge(selb_ready, g + 1)
                pe.wait_ge(selt_copied, g + 1)
                pe.nop(nofuse=True)
                for j in range(TILES):
                    ins = pe.transpose(ps_selt[0:WINDOW, j * P:(j + 1) * P], sel_b[:, slot % 2, j, :], ident_b[:, :])
                ins.then_inc(selt_done, 1)

            def products(g, q, trip):
                pe.wait_ge(ld_grp[q], 32 * trip + 32)
                pe.wait_ge(selt_copied, g + 2)
                pe.wait_ge(summed, g + RING - 1)
                for j in range(TILES):
                    ins = pe.matmul(ps_pre[q % 2][:, j * H:(j + 1) * H], lhs[0:WINDOW + De, q, j * P:(j + 1) * P],
                                    rhs[0:WINDOW + De, q, :], start=True, stop=True)
                ins.then_inc(pre_done, 1)

            def fast_layer0():
                pe.wait_ge(viol_ready, 3)
                pe.matmul(ps_sums[1][:, 0:2 * WINDOW], ones[0:1, :], zero_r[:, 0:2 * WINDOW], start=True, stop=True,
                          skip_group_check=True).then_inc(agg_done, 1)
                sel_transposed(0, 0)
                products(0, 0, 0)
                with pe.Fori(0, NI) as i:
                    for q in range(RING):
                        g = i * RING + q
                        sel_transposed(g + 1, (q + 1) % RING)
                        pe.wait_ge(hot_ready, 2 * g + 2)
                        hist(q % 2, hist_done)
                        products(g + 1, (q + 1) % RING, i + (q + 1) // RING)
                        pe.wait_ge(hid_ready, g + 1)
                        pe.wait_ge(added, g + 2)
                        for j in range(TILES):
                            for f in range(0, H, H // 2):
                                pe.matmul(ps_sums[q % 2][f:f + H // 2, 0:WINDOW], hid[:, q % 2, j, f:f + H // 2], sel[:, q, j, :],
                                          start=(j == 0), stop=(j == TILES - 1), skip_group_check=True)
                            ins = pe.matmul(ps_sums[q % 2][:, WINDOW:2 * WINDOW], ones_b[:, :], sel_b[:, q % 2, j, :],
                                            start=False, stop=(j == TILES - 1), skip_group_check=True)
                        ins.then_inc(agg_done, 1)

            def general_layer(L):
                s, width = gen[L], (H + 1, D)[L]
                val = hid[:, 0, 0:2, :].rearrange("p j f -> p (j f)") if L == 0 else gathered_h[:, 0, 0, :]
                with pe.Fori(0, NG) as g:
                    pe.wait_ge(s["ld"], (48, 32)[L] * g + (48, 32)[L])
                    if L == 0:
                        pe.wait_ge(s["hot"], 2 * g + 2)
                        hist(0, s["hist"])
                    for j in range(TILES):
                        pe.wait_ge(s["dstf"], g * TILES + j + 1)
                        pe.matmul(ps_t[:, 0:P], small[:, 4:5].broadcast_to([P, P]), ident[:, :], start=True, stop=True).then_inc(s["dstt"], 1)
                        if L == 0:
                            pe.matmul(ps_pre[0][:, 0:H], lhs[WINDOW:WINDOW + De, 0, j * P:(j + 1) * P], rhs[WINDOW:WINDOW + De, 0, :],
                                      start=True, stop=True).then_inc(s["eadot"], 1)
                        pe.wait_ge(s["sel"], (2 * TILES if L == 0 else TILES) * g + (2 if L == 0 else 1) * (j + 1))
                        pe.wait_ge(s["gat"], ((32 * TILES) if L == 0 else 16 * TILES) * g + (32 if L == 0 else 16) * (j + 1))
                        pe.matmul(ps_agg[:, 0:width], gathered[:, 1, 0, :], val[:, 0:width], start=True, stop=True).then_inc(s["comb"], 1)
                with pe.Fori(0, NT) as t:
                    pe.wait_ge(s["fold_ld"], 16 * t + 16)
                    pe.nop(nofuse=True)
                    if L == 0:
                        pe.transpose(ps_t[:, 0:P], gathered[:, 0, 0, :], ident[:, :])
                        pe.wait_ge(s["fold_diag"], t + 1)
                        pe.matmul(ps_t[:, P:2 * P], ones[:, :], gathered[:, 1, 0, :], start=True, stop=True).then_inc(s["fold_t"], 1)
                    else:
                        pe.transpose(ps_t[0:D, 0:P], gathered_h[:, 0, 0, :], ident[:, :]).then_inc(s["fold_t"], 1)

            open_hist()
            general = load_flag(pe, 0)
            with pe.If(general > 0):
                general_layer(0)
            with pe.Else():
                fast_layer0()
            pe.matmul(ps_deg[:, 0:NT], ones[0:1, :], zero_r[:, 0:NT], start=False, stop=True,
                      skip_group_check=True).then_inc(hist_closed, 1)

            pe.wait_ge(edges_done, 1)
            with pe.Fori(0, NCH) as i:
                for k in range(SLOTS):
                    c = i * SLOTS + k
                    pe.wait_ge(nu_mc, c + 1)
                    pe.matmul(ps_pre[0][0:D, 0:CW], w2[:, :], table[:, 0, bass.ds(c * CW, CW)], start=True, stop=True).then_inc(nu_m, 1)
                    pe.wait_ge(nu_ld[k], 16 * i + 16)
                    pe.wait_ge(nu_uc, c + 1)
                    pe.matmul(ps_pre[1][:, 0:CW], u1a[:, :], hl[:, k, :], start=True, stop=False)
                    pe.wait_ge(nu_mc, c + 2)
                    pe.matmul(ps_pre[1][:, 0:CW], u1b[:, :], mtc, start=False, stop=True).then_inc(nu_u, 1)
                    pe.wait_ge(nu_uc, c + 2)
                    pe.wait_ge(nu_x, c + 1)
                    for t in range(CHUNK):
                        o = ps_agg[:, t * D:(t + 1) * D]
                        pe.matmul(o, utc[:, t * P:(t + 1) * P], u2[:, :], start=True, stop=False)
                        ins = pe.matmul(o, ones[0:1, :], ub2_r[:, :], start=False, stop=True)
                    ins.then_inc(nu_y, 1)

            def fast_layer1():
                blocks = 10

                def half_product(slot, first, last):
                    for t in range(first, last):
                        ins = pe.matmul(ps_t[0:V, 0:3 * D], counts[:, slot, t, :], parts[:, t, :, :].rearrange("p a d -> p (a d)"),
                                        start=(t == 0), stop=(t == HI - 1))
                    if last == HI:
                        ins.then_inc(dense_done, 1)

                pe.wait_ge(parts_ready, 1)
                pe.matmul(ps_win, zero_r[0:1, 0:D], zero_r[0:1, 0:REACH], start=True, stop=True).then_inc(win_done, 1)
                with pe.Fori(0, NI1) as i:
                    for hf in range(2):
                        h = 2 * i + hf
                        for tile in range(HALF):
                            if tile % TILES == 0:
                                k = tile // TILES
                                q = 2 * hf + k
                                pe.wait_ge(sel1_ready, 2 * h + k + 1)
                                pe.wait_ge(gat1[q], 16 * TILES * i + 16 * TILES)
                                pe.wait_ge(table_added, 3 * h + 2 * k + 1 - k)
                                for j in range(TILES):
                                    ins = pe.matmul(ps_agg[0:D, 0:WINDOW], ring1[:, q, j, :], sel[:, k, j, :],
                                                    start=(j == 0), stop=(j == TILES - 1))
                                ins.then_inc(agg1_done, 1)
                                pe.wait_ge(hotlo_ready, 2 * h + k + 1)
                            pe.wait_ge(code_ready, h * HALF + tile + 1)
                            pe.wait_ge(count_copied, h * HALF + tile + 1)
                            for b in range(2):
                                w = HI // 2 * SPAN
                                ins = pe.matmul(ps_pre[tile % 2][:, 512 * b:512 * b + w], hot_lo[:, tile // TILES, tile % TILES, :],
                                                hot_code[:, tile % CODES, b * w:(b + 1) * w], start=True, stop=True)
                            ins.then_inc(count_done, 1)
                            if tile == 1:
                                pe.wait_ge(count_copied, h * HALF + 2)
                            if 1 <= tile <= blocks:
                                half_product(1 - hf, HI * (tile - 1) // blocks, HI * tile // blocks)
                        pe.wait_ge(reduced, h + 1)
                        pe.wait_ge(table_added, 3 * h + 3)
                        pe.matmul(ps_win, summed_rows, place, start=True, stop=True).then_inc(win_done, 1)
                pe.wait_ge(count_copied, NH * HALF + 2)
                half_product(1, 0, HI)
                pe.wait_ge(reduced, NH + 1)
                pe.wait_ge(table_added, 3 * NH + 2)
                pe.matmul(ps_win, summed_rows, place, start=True, stop=True).then_inc(win_done, 1)

            pe.wait_ge(in_ready, 1)
            general = load_flag(pe, 1)
            with pe.If(general > 0):
                general_layer(1)
            with pe.Else():
                fast_layer1()
            pe.wait_ge(edges1_done, 1)
            with pe.Fori(0, NCH) as i:
                for k in range(SLOTS):
                    c = i * SLOTS + k
                    pe.wait_ge(fin_scaled, c + 1)
                    pe.wait_ge(fin_x, c + 1)
                    pe.nop(nofuse=True)
                    for t in range(CHUNK):
                        ins = pe.transpose(ps_fin[k][:, t * P:(t + 1) * P], fin_stage[:, k, t * P:(t + 1) * P], ident[:, :])
                    ins.then_inc(fin_t, 1)


_OUT = "out_dram"


def kernel(x, src, dst, edge_attr_32, L0_gnn_mW1, L0_gnn_mb1, L0_gnn_mW2, L0_gnn_mb2, L0_gnn_uW1, L0_gnn_ub1,
           L0_gnn_uW2, L0_gnn_ub2):
    import concourse.bacc as bacc
    from concourse.bass_utils import run_bass_kernel_spmd

    x, src, dst, ea = (np.asarray(a) for a in (x, src, dst, edge_attr_32))
    n, d = x.shape
    e, de = ea.shape
    nt, ng = padded_sizes(n, e)
    x_t = np.zeros((nt * P, d), x.dtype)
    x_t[:n] = x
    x_t = np.ascontiguousarray(x_t.reshape(nt, P, d).transpose(1, 0, 2))

    def columns(a):
        p = np.full(ng * GROUP, n, a.dtype)
        p[:e] = a
        return np.ascontiguousarray(p.reshape(ng * TILES, P).T)

    ea_t = np.zeros((de, (ng + 1) * GROUP), ea.dtype)
    ea_t[:, :e] = ea.T
    arrays = {"x_t": x_t, "src_t": columns(src), "dst_t": columns(dst), "ea_t": ea_t}
    for name, w in (("mW1", L0_gnn_mW1), ("mb1", L0_gnn_mb1), ("mW2", L0_gnn_mW2), ("mb2", L0_gnn_mb2),
                    ("uW1", L0_gnn_uW1), ("ub1", L0_gnn_ub1), ("uW2", L0_gnn_uW2), ("ub2", L0_gnn_ub2)):
        arrays[name] = np.ascontiguousarray(w)
    nc = bacc.Bacc("TRN2", target_bir_lowering=False, num_devices=1)
    args = [nc.dram_tensor(k, a.shape, mybir.dt.from_np(a.dtype), kind="ExternalInput").ap() for k, a in arrays.items()]
    out = nc.dram_tensor(_OUT, x_t.shape, F32, kind="ExternalOutput").ap()
    bass_preln_mpnn_lightgcn(nc, *args, out, n, e)
    got = run_bass_kernel_spmd(nc, [arrays], core_ids=[0]).results[0][_OUT]
    return got.transpose(1, 0, 2).reshape(nt * P, d)[:n]
```

```python
from contextlib import ExitStack

import numpy as np

import concourse.bass as bass
from concourse import mybir

F32 = mybir.dt.float32
BF16 = mybir.dt.bfloat16
F16 = mybir.dt.float16
U8 = mybir.dt.uint8
I32 = mybir.dt.int32
ALU = mybir.AluOpType
ACT = mybir.ActivationFunctionType
AX = mybir.AxisListType

P = 128
TILES = 8
GROUP = P * TILES
RING = 4
WINDOW = 64
HALF = 2 * TILES
SPAN = 7
REACH = 96
CODES = 4
CHUNK = 3
ROWS = 96
SLOTS = 3
EPS = 1e-5


def padded_sizes(n_nodes, n_edges):
    per = CHUNK * SLOTS
    tiles = -(-(n_nodes + REACH) // P)
    groups = -(-n_edges // GROUP)
    return -(-tiles // per) * per, -(-groups // (2 * RING)) * 2 * RING


def bass_preln_mpnn_lightgcn(nc, x_t, src_t, dst_t, ea_t, mW1, mb1, mW2, mb2, uW1, ub1, uW2, ub2, out_t,
                             n_nodes, n_edges):
    _, NT, D = x_t.shape
    T = src_t.shape[1]
    NG = T // TILES
    NI = -(-n_edges // (GROUP * RING))
    N0 = NI * RING
    NI1 = NG // (2 * RING)
    NH = 2 * NI1
    G1 = NG // 2
    T1 = G1 * TILES
    HI = 2 * (n_nodes // (2 * P) + 1)
    V = HALF * SPAN
    De = ea_t.shape[0]
    H = mW1.shape[1]
    NP = NT * P
    NCH = NT // CHUNK // SLOTS
    CW = CHUNK * P
    NC = NCH * SLOTS
    TRIPS = [NCH * k // 3 for k in range(4)]
    PARTS = [(TRIPS[k] * SLOTS * CHUNK, TRIPS[k + 1] * SLOTS * CHUNK) for k in range(3)]
    assert H == P and D + D + De == mW1.shape[0] and D == WINDOW and WINDOW + De <= P
    assert NT <= P and HI <= NT and HI // 2 * SPAN <= 512 and V <= P
    assert T <= NP // 2 and 3 * T + SLOTS * CHUNK * 2 * H <= NP and NH <= 256 and NCH >= 3

    table_a = nc.dram_tensor("table_a", (NP, H), F32).ap()
    table_b = nc.dram_tensor("table_b", (NP, H), F32).ap()
    table_h = nc.dram_tensor("table_h", (NP, D), F32).ap()
    ht_dram = nc.dram_tensor("ht_dram", (D, NP), F32).ap()
    sums = [nc.dram_tensor("sums_0", (NP + P, H + 1), F32).ap(),
            nc.dram_tensor("sums_1", (NP + P, D), F32).ap()]

    with ExitStack() as ctx:
        def sb(name, shape, dt=F32):
            return ctx.enter_context(nc.sbuf_tensor(name, shape, dt))

        def ps(name, banks):
            return ctx.enter_context(nc.psum_tensor(name, [P, banks * 512], F32))

        def sem(name):
            return ctx.enter_context(nc.semaphore(name))

        x = sb("x", [P, NT, D])
        work = sb("work", [P, max(2 * RING * TILES * P, HI * 3 * D // 2)])
        table = sb("table", [P, 2, NP])
        dst_rel = sb("dst_rel", [P, T + TILES], U8)
        src_hi = sb("src_hi", [P, T + TILES], U8)
        src_lo = sb("src_lo", [P, T + TILES], U8)
        code = sb("code", [P, T - T1 + TILES], F16)
        node_of = sb("node_of", [V, NH + 1])
        bases = sb("bases", [1, NG + 2], I32)
        idx = sb("idx", [P, RING, TILES], I32)
        rhs = sb("rhs", [P, RING, H])
        sel = sb("sel", [P, RING, TILES, WINDOW])
        sel_b = sb("sel_b", [P, 2, TILES, WINDOW], BF16)
        hot_hi = sb("hot_hi", [P, 2, TILES, NT], BF16)
        hot_lo = sb("hot_lo", [P, 2, TILES, P], BF16)
        hid = sb("hid", [P, 2, TILES, H])
        ident = sb("ident", [P, P])
        ident_b = sb("ident_b", [P, P], BF16)
        ones = sb("ones", [P, P])
        ones_b = sb("ones_b", [P, P], BF16)
        iota_f = sb("iota_f", [P, P])
        iota_b = sb("iota_b", [P, P], BF16)
        w2 = sb("w2", [H, D])
        u1 = sb("u1", [2 * D, H])
        u2 = sb("u2", [H, D])
        mb2_c = sb("mb2_c", [D, 1])
        ub1_c = sb("ub1_c", [H, 1])
        ub2_r = sb("ub2_r", [1, D])
        inv_out = sb("inv_out", [P, NT])
        zero_r = sb("zero_r", [1, P])
        eps_c = sb("eps_c", [P, 1])
        small = sb("small", [P, 16])
        flag_i = sb("flag_i", [1, 2], I32)

        CONSTS = 8 + SPAN - 1
        SPREADS = -(-(T - T1) // 1024) + 4
        sel_flat = sel[:, :, :, :].rearrange("p a j n -> p (a j n)")
        hid_flat = hid[:, :, :, :].rearrange("p a j f -> p (a j f)")
        hot_lo_f = hot_lo[:, :, :, :].rearrange("p a j n -> p (a j n)").bitcast(F32)
        mean = hot_lo_f[:, 0:NT]
        rstd = hot_lo_f[:, NT:2 * NT]
        firsts = hot_lo_f[:, 2 * NT:2 * NT + NG + NH]
        iota_i = sel_flat[:, 0:P].bitcast(I32)
        w1ab = sel_flat[0:ROWS, P:P + 2 * H]
        tile_row = hid_flat[0:1, 0:HALF * (V + SPAN)]
        mod_row = hid_flat[0:1, HALF * (V + SPAN):HALF * (V + SPAN) + V]
        h2 = table[:, 1, 0:NT * D].rearrange("p (t d) -> p t d", d=D)
        square2 = table[:, 1, NT * D:2 * NT * D].rearrange("p (t d) -> p t d", d=D)
        parts = work[:, 0:HI * 3 * D // 2].bitcast(BF16).rearrange("p (t a d) -> p t a d", a=3, d=D)
        counts = table[:, 1, 0:HI * V].bitcast(BF16).rearrange("p (a t v) -> p a t v", a=2, t=HI)
        hot_code = table[:, 1, HI * V:HI * V + CODES * HI * SPAN // 2].bitcast(BF16).rearrange(
            "p (r c) -> p r c", r=CODES)
        ring1 = hid_flat.rearrange("p (r j f) -> p r j f", r=RING, j=TILES)
        iota_c = hot_hi[:, :, :, :].rearrange("p a j t -> p (a j t)")[:, 0:HI * SPAN].bitcast(F16)
        iota_ci = work[:, 2 * RING * TILES * P - HI * SPAN:2 * RING * TILES * P].bitcast(I32)
        summed_rows = rhs[0:V, 0, 0:D]
        code_s = rhs[:, 2, 0:2 * TILES].rearrange("p (a j) -> p a j", a=2)
        place = rhs[0:V, 1, 0:REACH]
        h = work[:, 0:NT * D].rearrange("p (t d) -> p t d", d=D)
        square = table[:, 1, NT * D:2 * NT * D].rearrange("p (t d) -> p t d", d=D)
        src_i = table[:, 1, 0:T].bitcast(I32)
        shifted = table[:, 0, NP - T:NP].bitcast(I32)
        dst_i = shifted
        dst_f = table[:, 0, 0:T]
        rel_tile = table[:, 0, T:T + T - T1]
        rel_half = table[:, 0, 2 * T - T1:3 * T - 2 * T1]
        gathered = work[:, 0:RING * GROUP].rearrange("p (r j f) -> p r j f", r=RING, j=TILES)
        lhs = work[:, RING * GROUP:2 * RING * GROUP].rearrange("p (r e) -> p r e", r=RING)
        gathered_h = work[:, 0:RING * TILES * D].rearrange("p (r j f) -> p r j f", r=RING, j=TILES)
        htc = hid[:, :, :, :].rearrange("p a j f -> p (a j f)")[0:ROWS, 0:SLOTS * CW].rearrange(
            "p (s n) -> p s n", s=SLOTS)
        abc = table[:, 0, 2 * T:2 * T + SLOTS * CHUNK * 2 * H].rearrange("p (s c f) -> p s c f", s=SLOTS, c=CHUNK)
        utc = sel_flat[:, 0:SLOTS * CW].rearrange("p (s n) -> p s n", s=SLOTS)
        h_stage = work[:, NT * D:NT * D + SLOTS * CHUNK * D].rearrange("p (s c f) -> p s c f", s=SLOTS, c=CHUNK)
        fin_stage = work[:, 0:SLOTS * CW].rearrange("p (s n) -> p s n", s=SLOTS)
        row_squares = work[:, SLOTS * CW:SLOTS * CW + SLOTS * CHUNK * D].rearrange("p (s c d) -> p s c d", s=SLOTS, c=CHUNK)
        cat = work[:, 0:SLOTS * CW].rearrange("p (s n) -> p s n", s=SLOTS)

        ps_t = ps("ps_t", 1)
        ps_pair = ps("ps_pair", 2)
        ps_selt_f, ps_agg = ps_pair[:, 0:512], ps_pair[:, 512:1024]
        ps_selt = ps_selt_f[:, :].bitcast(BF16)
        ps_win = ps_selt_f[0:D, 0:REACH]
        ps_pre = [ps("ps_pre0", 2), ps("ps_pre1", 2)]
        ps_deg = ps("ps_deg", 1)
        ps_rows = [ps_pre[0], ps_pre[1], ps_pair]
        ps_m = [ps_pre[0][:, 0:512], ps_pre[0][:, 512:1024], ps_pre[1][:, 0:512]]
        ps_u = [ps_pre[1][:, 512:1024], ps_agg, ps_t]
        ps_fin = [ps_t, ps_agg, ps_deg]
        ps_sums = [ps_agg, ps_t]

        ld_dst = sem("ld_dst")
        ld_src_all = sem("ld_src_all")
        ld_x = [sem(f"ld_x{k}") for k in range(3)]
        ld_w = sem("ld_w")
        const_made = sem("const_made")
        pool_step = sem("pool_step")
        w1ab_clear = sem("w1ab_clear")
        spread = sem("spread")
        dve_step = sem("dve_step")
        viol_ready = sem("viol_ready")
        viol_t = sem("viol_t")
        flag_ready = sem("flag_ready")
        bias_t = sem("bias_t")
        centred = sem("centred")
        squared = sem("squared")
        var_ready = sem("var_ready")
        std_ready = sem("std_ready")
        h_ready = sem("h_ready")
        table_clear = sem("table_clear")
        np_h = sem("np_h")
        np_t = sem("np_t")
        np_tc = sem("np_tc")
        np_mm = sem("np_mm")
        np_c = sem("np_c")
        np_sth = [sem(f"np_sth{k}") for k in range(SLOTS)]
        np_st = [sem(f"np_st{k}") for k in range(SLOTS)]
        ld_grp = [sem(f"ld_grp{q}") for q in range(RING)]
        ld_src = [sem(f"ld_src{q}") for q in range(RING)]
        gat = [sem(f"gat{q}") for q in range(RING)]
        sel_ready = sem("sel_ready")
        selb_ready = sem("selb_ready")
        selt_done = sem("selt_done")
        selt_copied = sem("selt_copied")
        hot_ready = sem("hot_ready")
        hist_done = sem("hist_done")
        pre_done = sem("pre_done")
        summed = sem("summed")
        hid_ready = sem("hid_ready")
        agg_done = sem("agg_done")
        added = sem("added")
        gen = [{n: sem(f"gen{L}_{n}") for n in ("zero_made", "zero_st", "ld", "dstf", "gat", "dstt", "eadot", "sel", "row", "comb", "combc",
                                                "scat", "free", "hot", "hist", "fold_ld", "fold_diag", "fold_t", "fold_c")}
               for L in range(2)]
        edges_done = sem("edges_done")
        hist_closed = sem("hist_closed")
        nu_ld = [sem(f"nu_ld{k}") for k in range(SLOTS)]
        nu_m = sem("nu_m")
        nu_mc = sem("nu_mc")
        nu_u = sem("nu_u")
        nu_uc = sem("nu_uc")
        nu_y = sem("nu_y")
        nu_x = sem("nu_x")
        deg_ready = sem("deg_ready")
        deg_root = sem("deg_root")
        row_sum = sem("row_sum")
        row_centred = sem("row_centred")
        row_squared = sem("row_squared")
        row_var = sem("row_var")
        st_h = sem("st_h")
        iota_made = sem("iota_made")
        split = sem("split")
        parts_ready = sem("parts_ready")
        hotlo_ready = sem("hotlo_ready")
        staged = sem("staged")
        code_ready = sem("code_ready")
        count_done = sem("count_done")
        count_copied = sem("count_copied")
        dense_done = sem("dense_done")
        reduced = sem("reduced")
        win_done = sem("win_done")
        ld_src1 = [sem(f"ld_src1_{q}") for q in range(RING)]
        gat1 = [sem(f"gat1_{q}") for q in range(RING)]
        sel1_ready = sem("sel1_ready")
        agg1_done = sem("agg1_done")
        table_added = sem("table_added")
        edges1_done = sem("edges1_done")
        in_ready = sem("in_ready")
        in_root = sem("in_root")
        fin_staged = sem("fin_staged")
        fin_root = sem("fin_root")
        fin_t = sem("fin_t")
        fin_x = sem("fin_x")
        st_out = sem("st_out")

        def load_flag(eng, L):
            eng.wait_ge(flag_ready, 1)
            return eng.value_load(flag_i[0:1, L:L + 1], min_val=0, max_val=1)

        def pipelined(eng, stages, lag):
            peeled = -(-lag // SLOTS)
            for s in range(peeled * SLOTS):
                stages(s, s % SLOTS, s // SLOTS, lambda d, s=s: s >= d)
            with eng.Fori(peeled, NCH) as i:
                for k in range(SLOTS):
                    stages(i * SLOTS + k, k, i, lambda d: True)
            for s in range(NC, NC + lag):
                stages(s, s % SLOTS, s // SLOTS, lambda d, s=s: s - d < NC)

        block = ctx.enter_context(nc.Block())

        @block.sync
        def _(sp):
            sp.dma_start(dst_i, dst_t).then_inc(ld_dst, 16)
            for k, (a, b) in enumerate(PARTS):
                sp.dma_start(x[:, a:b, :], x_t[:, a:b, :]).then_inc(ld_x[k], 16)
            sp.dma_start(w1ab[0:D, 0:H], mW1[0:D, :]).then_inc(ld_w, 16)
            sp.dma_start(w1ab[0:D, H:2 * H], mW1[D:2 * D, :]).then_inc(ld_w, 16)
            sp.wait_ge(w1ab_clear, 1)
            sp.dma_start(w1ab[D:D + 1, H:2 * H], mb1.rearrange("(a f) -> a f", a=1)).then_inc(ld_w, 16)
            for q in range(RING):
                sp.dma_start(rhs[WINDOW:WINDOW + De, q, :], mW1[2 * D:2 * D + De, :]).then_inc(ld_w, 16)
            sp.dma_start(w2[:], mW2).then_inc(ld_w, 16)
            sp.dma_start(u1[0:D, :], uW1[D:2 * D, :]).then_inc(ld_w, 16)
            sp.dma_start(u1[D:2 * D, :], uW1[0:D, :]).then_inc(ld_w, 16)
            sp.dma_start(u2[:], uW2).then_inc(ld_w, 16)
            sp.dma_start(mb2_c[:], mb2.rearrange("(f a) -> f a", a=1)).then_inc(ld_w, 16)
            sp.dma_start(ub1_c[:], ub1.rearrange("(f a) -> f a", a=1)).then_inc(ld_w, 16)
            sp.dma_start(ub2_r[:], ub2.rearrange("(a f) -> a f", a=1)).then_inc(ld_w, 16)

            sp.dma_start(src_i, src_t).then_inc(ld_src_all, 16)

            a_rows = table_a.rearrange("(t p) f -> p t f", p=P)
            b_rows = table_b.rearrange("(t p) f -> p t f", p=P)

            def projected(s, k, i, run):
                if run(0):
                    sp.wait_ge(np_tc, s + 2)
                    sp.dma_start(ht_dram[:, bass.ds(s * CW, CW)], htc[0:D, k, :]).then_inc(np_sth[k], 16)
                if run(1):
                    b, tiles = (k + SLOTS - 1) % SLOTS, bass.ds((s - 1) * CHUNK, CHUNK)
                    sp.wait_ge(np_c, s + SLOTS)
                    sp.dma_start(a_rows[:, tiles, :], abc[:, b, :, 0:H]).then_inc(np_st[b], 16)
                    sp.dma_start(b_rows[:, tiles, :], abc[:, b, :, H:2 * H]).then_inc(np_st[b], 16)

            pipelined(sp, projected, 1)
            for k in range(SLOTS):
                sp.wait_ge(np_sth[k], 16 * NCH + 16)
                sp.wait_ge(np_st[k], 32 * NCH + 32)

            def group_loads():
                def operands(g, q):
                    base = sp.value_load(bases[0:1, bass.ds(g + 1, 1)], min_val=0, max_val=n_nodes)
                    sp.wait_ge(pre_done, g + 1)
                    sp.dma_start(lhs[WINDOW:WINDOW + De, q, :], ea_t[:, bass.ds(g * GROUP, GROUP)]).then_inc(ld_grp[q], 16)
                    sp.dma_start(rhs[0:WINDOW, q, :], table_b[bass.ds(base, WINDOW), :]).then_inc(ld_grp[q], 16)

                with sp.Fori(0, NI) as i:
                    for q in range(RING):
                        g = i * RING + q
                        operands(g, q)
                        sp.wait_ge(summed, g + 1)
                        sp.dma_start(idx[:, q, :], src_t[:, bass.ds(g * TILES, TILES)]).then_inc(ld_src[q], 16)
                operands(N0, 0)

            def general_loads(L):
                s, width = gen[L], (H + 1, D)[L]
                zero = hid[:, 0, 0:2, :].rearrange("p j f -> p (j f)")[:, 0:width]
                rows = sums[L].rearrange("(t p) f -> p t f", p=P)
                sp.wait_ge(s["zero_made"], 1)
                with sp.Fori(0, NT + 1) as t:
                    sp.dma_start(rows[:, bass.ds(t, 1), :], zero.unsqueeze(1)).then_inc(s["zero_st"], 16)
                with sp.Fori(0, NG) as g:
                    sp.wait_ge(s["free"], g * TILES + 1)
                    sp.nop(nofuse=True)
                    sp.dma_start(idx[:, 0, :], src_t[:, bass.ds(g * TILES, TILES)]).then_inc(s["ld"], 16)
                    sp.dma_start(idx[:, 1, :], dst_t[:, bass.ds(g * TILES, TILES)]).then_inc(s["ld"], 16)
                    if L == 0:
                        sp.dma_start(lhs[WINDOW:WINDOW + De, 0, :], ea_t[:, bass.ds(g * GROUP, GROUP)]).then_inc(s["ld"], 16)
                sp.wait_ge(s["free"], NG * TILES + 1)
                with sp.Fori(0, NT) as t:
                    sp.wait_ge(s["fold_c"], t + 1)
                    sp.dma_start(gathered[:, 0, 0:2, :].rearrange("p j f -> p (j f)")[:, 0:width].unsqueeze(1),
                                 rows[:, bass.ds(t, 1), :]).then_inc(s["fold_ld"], 16)

            general = load_flag(sp, 0)
            with sp.If(general > 0):
                general_loads(0)
            with sp.Else():
                group_loads()

            sp.wait_ge(edges_done, 1)
            with sp.Fori(0, NCH) as i:
                for k in range(SLOTS):
                    c = i * SLOTS + k
                    sp.wait_ge(nu_u, c + 1)
                    sp.dma_start(cat[D:P, k, :], ht_dram[:, bass.ds(c * CW, CW)]).then_inc(nu_ld[k], 16)
            for k, (a, b) in enumerate(PARTS):
                sp.wait_ge(h_ready, 3 + k + 1)
                sp.dma_start(table_h.rearrange("(t p) f -> p t f", p=P)[:, a:b, :], h2[:, a:b, :]).then_inc(st_h, 16)

            def source_loads():
                with sp.Fori(0, NI1) as i:
                    for q in range(RING):
                        g = i * RING + q
                        sp.wait_ge(agg1_done, g + 1)
                        sp.dma_start(idx[:, q, :], src_t[:, bass.ds(g * TILES, TILES)]).then_inc(ld_src1[q], 16)

            sp.wait_ge(st_h, 48)
            general = load_flag(sp, 1)
            with sp.If(general > 0):
                general_loads(1)
            with sp.Else():
                source_loads()

            for k, (a, b) in enumerate(PARTS):
                sp.wait_ge(fin_x, SLOTS * TRIPS[k + 1] + SLOTS)
                sp.dma_start(out_t[:, a:b, :], x[:, a:b, :]).then_inc(st_out, 16)
            sp.wait_ge(st_out, 48)

        @block.gpsimd
        def _(pool):
            pool.memset(ones[:], 1.0).then_inc(const_made, 1)
            pool.memset(ident[:], 0.0).then_inc(pool_step, 1)
            pool.wait_ge(pool_step, 1)
            pool.affine_select(out=ident[:], in_=ident[:], compare_op=ALU.not_equal, fill=1.0, base=0,
                               pattern=[[-1, P]], channel_multiplier=1).then_inc(const_made, 1)
            pool.iota(iota_i[:], pattern=[[1, P]], base=0, channel_multiplier=0).then_inc(const_made, 1)
            pool.memset(eps_c[:], EPS).then_inc(const_made, 1)
            for part in range(3):
                pool.wait_ge(h_ready, part + 1)
                with pool.Fori(TRIPS[part], TRIPS[part + 1]) as i:
                    for k in range(SLOTS):
                        c = i * SLOTS + k
                        pool.wait_ge(np_t, c + 1)
                        pool.tensor_copy(h_stage[:, k, :, :], h[:, bass.ds(c * CHUNK, CHUNK), :]).then_inc(np_h, 1)
            for k in range(SLOTS):
                pool.wait_ge(np_st[k], 32 * NCH + 32)

            def gathers(trips, rows, ring, loaded, done, freed):
                with pool.Fori(0, trips) as i:
                    for q in range(RING):
                        pool.wait_ge(loaded[q], 16 * i + 16)
                        pool.wait_ge(freed, i * RING + q + 1)
                        pool.nop(nofuse=True)
                        for j in range(TILES):
                            pool.indirect_dma_start(ring[:, q, j, :], None, rows,
                                                    bass.IndirectOffsetOnAxis(ap=idx[:, q, j:j + 1], axis=0)
                                                    ).then_inc(done[q], 16)

            def general_gathers(L):
                s, width = gen[L], (H + 1, D)[L]
                pool.wait_ge(s["zero_st"], 16 * (NT + 1))
                with pool.Fori(0, NG) as g:
                    pool.wait_ge(s["ld"], (48, 32)[L] * g + (48, 32)[L])
                    pool.nop(nofuse=True)
                    for j in range(TILES):
                        if L == 0:
                            pool.indirect_dma_start(gathered[:, 0, 0, :], None, table_a,
                                                    bass.IndirectOffsetOnAxis(ap=idx[:, 0, j:j + 1], axis=0)).then_inc(s["gat"], 16)
                            pool.indirect_dma_start(gathered[:, 0, 1, :], None, table_b,
                                                    bass.IndirectOffsetOnAxis(ap=idx[:, 1, j:j + 1], axis=0)).then_inc(s["gat"], 16)
                        else:
                            pool.indirect_dma_start(gathered_h[:, 0, 0, :], None, table_h,
                                                    bass.IndirectOffsetOnAxis(ap=idx[:, 0, j:j + 1], axis=0)).then_inc(s["gat"], 16)
                        pool.wait_ge(s["combc"], g * TILES + j + 1)
                        pool.nop(nofuse=True)
                        pool.indirect_dma_start(sums[L], bass.IndirectOffsetOnAxis(ap=idx[:, 2, 0:1], axis=0),
                                                hid[:, 1, 0:2, :].rearrange("p j f -> p (j f)")[:, 0:width], None,
                                                compute_op=ALU.add).then_inc(s["scat"], 16)
                        pool.wait_ge(s["scat"], g * (16 * TILES) + 16 * j + 16)
                        pool.sem_inc(s["free"], 1)

            general = load_flag(pool, 0)
            with pool.If(general > 0):
                general_gathers(0)
            with pool.Else():
                gathers(NI, table_a, gathered, ld_src, gat, summed)
            pool.wait_ge(edges_done, 1)
            pool.iota(iota_ci, pattern=[[1, HI * SPAN]], base=0, channel_multiplier=0).then_inc(iota_made, 1)
            pool.wait_ge(iota_made, 1)
            pool.wait_ge(nu_x, NC)
            pool.memset(table[0:D, 0, :], 0.0).then_inc(in_ready, 1)
            pool.wait_ge(st_h, 48)
            general = load_flag(pool, 1)
            with pool.If(general > 0):
                general_gathers(1)
            with pool.Else():
                gathers(NI1, table_h, ring1, ld_src1, gat1, agg1_done)

        @block.scalar
        def _(act):
            def root(n, a, b):
                act.wait_ge(var_ready, n)
                act.activation(rstd[:, a:b], mean[:, a:b], ACT.Sqrt, bias=eps_c[:, 0:1], scale=1.0 / D).then_inc(std_ready, 1)

            act.wait_ge(const_made, CONSTS)
            act.wait_ge(viol_t, 1)
            for c in range(0, T - T1, 1024):
                n = min(1024, T - T1 - c)
                act.copy(rel_tile[:, c:c + n], ps_pre[c // 1024][:, 0:n]).then_inc(spread, 1)
            act.copy(firsts[:, 0:NG], ps_t[:, 0:NG]).then_inc(spread, 1)
            act.copy(firsts[:, NG:NG + NH], ps_agg[:, P:P + NH]).then_inc(spread, 1)
            act.copy(node_of[:, 1:NH + 1], ps_deg[0:V, 0:NH]).then_inc(spread, 1)
            act.copy(small[:, 5:6], ps_deg[:, 511:512]).then_inc(spread, 1)
            for k, (a, b) in enumerate(PARTS):
                act.wait_ge(centred, k + 1)
                act.activation(square[:, a:b, :], h[:, a:b, :], ACT.Square).then_inc(squared, 1)
            for k, (a, b) in enumerate(PARTS):
                root(k + 1, a, b)

            def projection(s, k, i, run):
                if run(0):
                    act.wait_ge(np_t, s + SLOTS + 1)
                    act.wait_ge(np_sth[k], 16 * i + 16)
                    if not isinstance(s, int):
                        act.wait_ge(np_mm, s - 2)
                    act.copy(htc[0:D, k, :], ps_t[0:D, 0:CW]).then_inc(np_tc, 1)
                if run(1):
                    b = (k + SLOTS - 1) % SLOTS
                    act.wait_ge(np_mm, s)
                    act.wait_ge(np_st[b], 32 * i + (32 if k else 0))
                    act.copy(abc[:, b, :, :], ps_rows[b][:, 0:CHUNK * 2 * H].rearrange("p (c f) -> p c f", c=CHUNK)).then_inc(np_c, 1)

            pipelined(act, projection, 1)
            act.wait_ge(flag_ready, 1)
            act.copy(table[:, 1, :], small[:, 7:8].broadcast_to([P, NP])).then_inc(table_clear, 1)

            def selt_copy(g, q):
                act.wait_ge(selt_done, g + 1)
                act.wait_ge(pre_done, g + 1)
                act.copy(lhs[0:WINDOW, q, :], ps_selt[0:WINDOW, 0:GROUP]).then_inc(selt_copied, 1)

            def sel_copy(g, slot):
                act.wait_ge(sel_ready, g + 1)
                act.wait_ge(agg_done, g + 3)
                act.copy(sel_b[:, slot % 2, :, :], sel[:, slot, :, :]).then_inc(selb_ready, 1)

            def fast_hidden():
                sel_copy(0, 0)
                selt_copy(0, 0)
                with act.Fori(0, NI) as i:
                    for q in range(RING):
                        g = i * RING + q
                        sel_copy(g + 1, (q + 1) % RING)
                        selt_copy(g + 1, (q + 1) % RING)
                        act.wait_ge(summed, g + RING + 1)
                        act.activation(hid[:, q % 2, :, :], hid[:, q % 2, :, :], ACT.Relu).then_inc(hid_ready, 1)

            general = load_flag(act, 0)
            with act.If(general > 0):
                act.nop()
            with act.Else():
                fast_hidden()

            act.wait_ge(deg_ready, 1)
            act.activation(inv_out[:], inv_out[:], ACT.Sqrt).then_inc(deg_root, 1)
            act.wait_ge(edges_done, 1)

            def update(s, k, i, run):
                if run(0):
                    act.wait_ge(nu_u, s + SLOTS + 1)
                    act.wait_ge(nu_y, s + 1)
                    act.activation(utc[:, k, :], ps_u[k][:, 0:CW], ACT.Relu, bias=ub1_c[:, 0:1]).then_inc(nu_uc, 1)
                if run(4):
                    act.wait_ge(row_centred, s - 3)
                    act.wait_ge(row_var, s - 3)
                    act.activation(row_squares[:, (k + 2) % SLOTS, :, :], h2[:, bass.ds((s - 4) * CHUNK, CHUNK), :], ACT.Square
                                   ).then_inc(row_squared, 1)

            pipelined(act, update, 4)
            root(4, 0, NT)
            act.wait_ge(in_ready, NC + 1)
            act.activation(table[D:P, 0, :], table[D:P, 0, :], ACT.Sqrt).then_inc(in_root, 1)

            def copy_counts():
                act.wait_ge(st_h, 48)
                act.wait_ge(parts_ready, 1)
                with act.Fori(0, NI1) as i:
                    for hf in range(2):
                        h = 2 * i + hf
                        act.wait_ge(dense_done, h + 1)
                        for tile in range(HALF):
                            act.wait_ge(count_done, h * HALF + tile + CODES + 1)
                            to = counts[:, hf, :, tile * SPAN:(tile + 1) * SPAN].rearrange("p (a b) n -> p a b n", a=2)
                            act.copy(to, ps_pre[tile % 2][:, :].rearrange("p (a x) -> p a x", a=2)[:, :, 0:HI // 2 * SPAN]
                                     .rearrange("p a (b n) -> p a b n", n=SPAN)).then_inc(count_copied, 1)

            general = load_flag(act, 1)
            with act.If(general > 0):
                act.nop()
            with act.Else():
                copy_counts()
            act.wait_ge(edges1_done, 1)
            with act.Fori(0, NCH) as i:
                for k in range(SLOTS):
                    c = i * SLOTS + k
                    act.wait_ge(fin_t, c + 1)
                    act.copy(fin_stage[:, k, :], table[:, 0, bass.ds(c * CW, CW)]).then_inc(fin_staged, 1)

        @block.vector
        def _(dve):
            steps = [0]

            def step(ins):
                steps[0] += 1
                ins.then_inc(dve_step, 1)
                dve.wait_ge(dve_step, steps[0])

            def across(column, n):
                return column.unsqueeze(2).broadcast_to([P, column.shape[1], n])

            def by(n, a):
                return a.rearrange("p (g j) -> p g j", j=n)

            def scaled_rows(rows, ready):
                for k, (a, b) in enumerate(PARTS):
                    ready(k, a, b)
                    dve.scalar_tensor_tensor(rows[:, a:b, :], rows[:, a:b, :], 0.0, across(rstd[:, a:b], D), ALU.max, ALU.mult).then_inc(h_ready, 1)

            def normalise():
                for k, (a, b) in enumerate(PARTS):
                    dve.wait_ge(ld_x[k], 16)
                    step(dve.tensor_reduce(mean[:, a:b], x[:, a:b, :], AX.X, ALU.add))
                    dve.scalar_tensor_tensor(h[:, a:b, :], across(mean[:, a:b], D), -1.0 / D, x[:, a:b, :], ALU.mult, ALU.add).then_inc(centred, 1)

                def factors(k, a, b):
                    dve.wait_ge(squared, k + 1)
                    dve.tensor_reduce(mean[:, a:b], square[:, a:b, :], AX.X, ALU.add).then_inc(var_ready, 1)
                    dve.wait_ge(std_ready, k + 1)
                    step(dve.reciprocal(rstd[:, a:b], rstd[:, a:b]))

                scaled_rows(h, factors)

            dve.memset(w1ab[D:ROWS, :], 0.0).then_inc(w1ab_clear, 1)
            step(dve.memset(htc[D:ROWS, :, :], 0.0))
            dve.memset(htc[D:D + 1, :, :], 1.0).then_inc(const_made, 1)
            dve.memset(zero_r[:], 0.0).then_inc(const_made, 1)
            dve.memset(node_of[:], 0.0).then_inc(const_made, 1)
            step(dve.memset(hid_flat[0:1, :], 0.0))
            step(dve.memset(tile_row[0:1, SPAN:V], -1.0))
            dve.memset(tile_row.rearrange("p (j x) -> p j x", x=V + SPAN)[:, 1:HALF, 0:SPAN], 1.0).then_inc(const_made, 1)
            for k in range(1, SPAN):
                dve.memset(mod_row.rearrange("p (j k) -> p j k", k=SPAN)[:, :, k:k + 1], float(k)).then_inc(const_made, 1)
            dve.wait_ge(const_made, CONSTS)
            dve.tensor_copy(iota_f[:], iota_i[:])
            dve.tensor_copy(iota_b[:], iota_i[:])
            dve.tensor_copy(ident_b[:], ident[:])
            dve.tensor_copy(ones_b[:], ones[:])
            dve.memset(dst_rel[:, T:T + TILES], 0)
            dve.memset(src_hi[:, T:T + TILES], 0)
            dve.memset(src_lo[:, T:T + TILES], 0)
            dve.memset(bases[0:1, 0:1], 0)
            dve.memset(bases[0:1, NG + 1:NG + 2], 0)
            dve.memset(small[:], 0.0)
            dve.memset(code[:, T - T1:T - T1 + TILES], 0.0)
            dve.wait_ge(ld_dst, 16)
            dve.tensor_copy(bases[0:1, 1:NG + 1], dst_i[0:1, 0:T:TILES])
            step(dve.tensor_copy(dst_f, dst_i))
            dve.sem_inc(viol_ready, 1)

            normalise()

            dve.wait_ge(spread, SPREADS)
            step(dve.tensor_tensor(rel_tile, dst_f[:, T1:T], rel_tile, ALU.subtract))
            step(dve.tensor_tensor(by(HALF, rel_half), by(HALF, dst_f[:, T1:T]),
                                   firsts[:, NG:NG + NH].unsqueeze(2).broadcast_to([P, NH, HALF]), ALU.subtract))
            step(dve.tensor_tensor(by(TILES, dst_f), by(TILES, dst_f),
                                   firsts[:, 0:NG].unsqueeze(2).broadcast_to([P, NG, TILES]), ALU.subtract))
            dve.wait_ge(ld_src_all, 16)
            step(dve.tensor_scalar(shifted, src_i, 7, None, ALU.arith_shift_right))
            step(dve.tensor_copy(src_hi[:, 0:T], shifted))
            step(dve.tensor_scalar(shifted, src_i, P - 1, None, ALU.bitwise_and))
            dve.tensor_copy(src_lo[:, 0:T], shifted)
            dve.tensor_copy(dst_rel[:, 0:T], dst_f)
            for rel, limit, o in ((dst_f, WINDOW, 0), (rel_tile, SPAN, 8), (rel_half, REACH, 11)):
                step(dve.tensor_reduce(small[:, o:o + 1], rel, AX.X, ALU.max))
                step(dve.tensor_reduce(small[:, o + 1:o + 2], rel, AX.X, ALU.min))
                step(dve.tensor_scalar(small[:, o:o + 1], small[:, o:o + 1], float(1 - limit), None, ALU.add))
                step(dve.scalar_tensor_tensor(small[:, o + 2:o + 3], small[:, o + 1:o + 2], -1.0, small[:, o:o + 1], ALU.mult, ALU.max))
            step(dve.tensor_tensor(small[:, 14:15], small[:, 10:11], small[:, 13:14], ALU.max))
            step(dve.tensor_tensor(small[:, 15:16], small[:, 14:15], small[:, 2:3], ALU.max))
            step(dve.tensor_scalar(rel_tile, rel_tile, -1.0, float(SPAN), ALU.max, ALU.min))
            step(dve.scalar_tensor_tensor(code[:, 0:T - T1], src_hi[:, T1:T], float(SPAN), rel_tile, ALU.mult, ALU.add))
            dve.wait_ge(bias_t, 1)
            step(dve.tensor_tensor(x[:], x[:], ps_deg[:, 256:256 + D].unsqueeze(1).broadcast_to([P, NT, D]), ALU.add))
            dve.sem_inc(viol_ready, 1)
            dve.wait_ge(viol_t, 2)
            step(dve.tensor_reduce(small[0:1, 8:10], ps_deg[0:1, 0:2 * P].rearrange("p (a n) -> p a n", a=2), AX.X, ALU.max))
            dve.tensor_scalar(flag_i[:], small[0:1, 8:10], 0.0, None, ALU.is_gt).then_inc(flag_ready, 1)
            for k in range(SLOTS):
                dve.wait_ge(np_st[k], 32 * NCH + 32)
            dve.memset(table[:, 0, :], 0.0).then_inc(table_clear, 1)

            iota_w = iota_b[:, 0:WINDOW].unsqueeze(1).broadcast_to([P, TILES, WINDOW])

            def make_sel(col, slot, ready):
                rel = dst_rel[:, bass.ds(col, TILES)].unsqueeze(2).broadcast_to([P, TILES, WINDOW])
                dve.tensor_tensor(sel[:, slot, :, :], rel, iota_w, ALU.is_equal).then_inc(ready, 1)

            def make_hot(col, slot, ready):
                hi = src_hi[:, bass.ds(col, TILES)].unsqueeze(2)
                lo = src_lo[:, bass.ds(col, TILES)].unsqueeze(2)
                dve.tensor_tensor(hot_hi[:, slot, :, :], hi.broadcast_to([P, TILES, NT]),
                                  iota_b[:, 0:NT].unsqueeze(1).broadcast_to([P, TILES, NT]), ALU.is_equal).then_inc(ready, 1)
                dve.tensor_tensor(hot_lo[:, slot, :, :], lo.broadcast_to([P, TILES, P]),
                                  iota_b[:, :].unsqueeze(1).broadcast_to([P, TILES, P]), ALU.is_equal).then_inc(ready, 1)

            def add_window(base, slot, rows, halves, done, n):
                dve.wait_ge(done, n)
                spot = table[0:rows, 0:halves, bass.ds(base, WINDOW)]
                new = ps_sums[slot][0:rows, 0:halves * WINDOW].rearrange("p (a n) -> p a n", a=halves)
                dve.tensor_tensor(spot, spot, new, ALU.add).then_inc(done, 1)

            def fast_layer0():
                dve.wait_ge(table_clear, 2)
                dve.wait_ge(agg_done, 1)
                make_sel(0, 0, sel_ready)
                dve.wait_ge(hist_done, 1)
                make_hot(0, 0, hot_ready)
                with dve.Fori(0, NI) as i:
                    for q in range(RING):
                        g = i * RING + q
                        base = dve.value_load(bases[0:1, bass.ds(g, 1)], min_val=0, max_val=n_nodes)
                        dve.wait_ge(agg_done, g + 2)
                        make_sel((g + 1) * TILES, (q + 1) % RING, sel_ready)
                        dve.wait_ge(hist_done, g + 2)
                        make_hot((g + 1) * TILES, (q + 1) % 2, hot_ready)
                        dve.wait_ge(pre_done, g + RING + 1)
                        dve.wait_ge(gat[q], 16 * TILES * i + 16 * TILES)
                        dve.wait_ge(agg_done, g + 3)
                        for half in range(2):
                            t0 = half * TILES // 2
                            ins = dve.tensor_tensor(
                                hid[:, q % 2, t0:t0 + TILES // 2, :], gathered[:, q, t0:t0 + TILES // 2, :],
                                ps_pre[q % 2][:, 512 * half:512 * half + 512].rearrange("p (j f) -> p j f", f=H), ALU.add)
                        ins.then_inc(summed, 1)
                        dve.wait_ge(agg_done, g + 4)
                        add_window(base, (q + 1) % 2, P, 2, added, g + 2)
                base = dve.value_load(bases[0:1, N0:N0 + 1], min_val=0, max_val=n_nodes)
                dve.wait_ge(agg_done, N0 + 4)
                add_window(base, (N0 + 1) % 2, P, 2, added, N0 + 2)
                dve.wait_ge(added, N0 + 3)

            def general_layer(L):
                s, width = gen[L], (H + 1, D)[L]
                if L == 0:
                    dve.wait_ge(table_clear, 2)
                dve.memset(hid[:, 0, 0:2, :], 0.0).then_inc(s["zero_made"], 1)
                dve.wait_ge(s["zero_st"], 16 * (NT + 1))
                val = hid[:, 0, 0:2, :].rearrange("p j f -> p (j f)")
                out_rows = hid[:, 1, 0:2, :].rearrange("p j f -> p (j f)")[:, 0:width]
                dstf, eq, low = small[:, 4:5], gathered[:, 1, 0, :], gathered[:, 1, 1, :]
                n = [0]

                def link(ins, g, sem_name="row", per=0):
                    n[0] += 1
                    ins.then_inc(s[sem_name], 1)
                    dve.wait_ge(s[sem_name], g * per + n[0])

                per_tile = 6 if L == 0 else 4
                dve.memset(val[:, H:H + 1], 1.0).then_inc(s["row"], 1)
                dve.wait_ge(s["row"], 1)
                n[0] = 1
                with dve.Fori(0, NG) as g:
                    dve.wait_ge(s["ld"], (48, 32)[L] * g + (48, 32)[L])
                    if L == 0:
                        dve.wait_ge(s["hist"], g + 1)
                        make_hot(g * TILES, 0, s["hot"])
                    for j in range(TILES):
                        dve.wait_ge(s["dstt"], g * TILES + j + 1)
                        dve.wait_ge(s["free"], g * TILES + j + 1)
                        dve.tensor_copy(dstf, idx[:, 1, j:j + 1]).then_inc(s["dstf"], 1)
                        dve.wait_ge(s["dstf"], g * TILES + j + 1)
                        dve.wait_ge(s["dstt"], g * TILES + j + 2)
                        link(dve.tensor_scalar(eq, ps_t[:, 0:P], dstf, None, ALU.is_equal), g, "row", per_tile * TILES)
                        link(dve.scalar_tensor_tensor(low, iota_f[:, :], small[:, 5:6], eq, ALU.is_lt, ALU.mult), g, "row", per_tile * TILES)
                        link(dve.tensor_reduce(small[:, 6:7], low, AX.X, ALU.max), g, "row", per_tile * TILES)
                        link(dve.scalar_tensor_tensor(small[:, 7:8], small[:, 5:6], float(NP), dstf, ALU.add, ALU.subtract), g, "row", per_tile * TILES)
                        dve.scalar_tensor_tensor(idx[:, 2, 0:1], small[:, 7:8], small[:, 6:7], dstf, ALU.mult, ALU.add).then_inc(s["sel"], 1)
                        dve.wait_ge(s["gat"], ((32 * TILES) if L == 0 else 16 * TILES) * g + (32 if L == 0 else 16) * (j + 1))
                        if L == 0:
                            dve.wait_ge(s["eadot"], g * TILES + j + 1)
                            link(dve.tensor_tensor(gathered[:, 0, 0, :], gathered[:, 0, 0, :], gathered[:, 0, 1, :], ALU.add), g, "row", per_tile * TILES)
                            link(dve.tensor_tensor(gathered[:, 0, 0, :], gathered[:, 0, 0, :], ps_pre[0][:, 0:H], ALU.add), g, "row", per_tile * TILES)
                            dve.tensor_scalar(val[:, 0:H], gathered[:, 0, 0, :], 0.0, None, ALU.max).then_inc(s["sel"], 1)
                        dve.wait_ge(s["comb"], g * TILES + j + 1)
                        dve.tensor_copy(out_rows, ps_agg[:, 0:width]).then_inc(s["combc"], 1)
                with dve.Fori(0, NT) as t:
                    dve.wait_ge(s["fold_ld"], 16 * t + 16)
                    if L == 0:
                        dve.tensor_scalar(eq, ident[:, :], gathered[:, 0, 1, 0:1], None, ALU.mult).then_inc(s["fold_diag"], 1)
                    dve.wait_ge(s["fold_t"], t + 1)
                    if L == 0:
                        dve.tensor_copy(table[:, :, bass.ds(t * P, P)],
                                        ps_t[:, 0:2 * P].rearrange("p (a n) -> p a n", a=2)).then_inc(s["fold_c"], 1)
                    else:
                        dve.tensor_copy(table[0:D, 0, bass.ds(t * P, P)], ps_t[0:D, 0:P]).then_inc(s["fold_c"], 1)
                dve.wait_ge(s["fold_c"], NT + 1)

            general = load_flag(dve, 0)
            with dve.If(general > 0):
                general_layer(0)
            with dve.Else():
                fast_layer0()
            dve.sem_inc(edges_done, 1)

            dve.wait_ge(hist_closed, 1)
            dve.tensor_scalar(inv_out[:], ps_deg[:, 0:NT], 1.0, None, ALU.max).then_inc(deg_ready, 1)
            dve.wait_ge(deg_root, 1)
            step(dve.reciprocal(inv_out[:], inv_out[:]))

            def tiles(c):
                return bass.ds(c * CHUNK, CHUNK)

            def update(s, k, i, run):
                cols, rows = bass.ds(s * CW, CW), bass.ds((s - 2) * CW, CW)
                if run(0):
                    dve.wait_ge(nu_m, s + 1)
                    dve.wait_ge(nu_u, s + 1)
                    dve.scalar_tensor_tensor(cat[0:D, k, :], table[0:D, 1, cols], mb2_c[:, 0:1], ps_m[k][0:D, 0:CW],
                                             ALU.mult, ALU.add).then_inc(nu_mc, 1)
                if run(2):
                    b = (k + 1) % SLOTS
                    dve.tensor_scalar(table[D:P, 0, rows], table[D:P, 1, rows], 1.0, None, ALU.max).then_inc(in_ready, 1)
                    dve.wait_ge(nu_y, s - 2 + SLOTS + 1)
                    dve.tensor_tensor(x[:, tiles(s - 2), :], x[:, tiles(s - 2), :],
                                      ps_m[b][:, 0:CHUNK * D].rearrange("p (c f) -> p c f", c=CHUNK), ALU.add).then_inc(nu_x, 1)
                if run(3):
                    dve.wait_ge(nu_x, s - 2)
                    dve.nop(nofuse=True)
                    dve.tensor_reduce(mean[:, tiles(s - 3)], x[:, tiles(s - 3), :], AX.X, ALU.add).then_inc(row_sum, 1)
                if run(4):
                    dve.wait_ge(row_sum, s - 3)
                    dve.scalar_tensor_tensor(h2[:, tiles(s - 4), :], across(mean[:, tiles(s - 4)], D), -1.0 / D, x[:, tiles(s - 4), :],
                                             ALU.mult, ALU.add).then_inc(row_centred, 1)
                if run(5):
                    dve.wait_ge(row_squared, s - 4)
                    dve.nop(nofuse=True)
                    dve.tensor_reduce(mean[:, tiles(s - 5)], row_squares[:, (k + 1) % SLOTS, :, :], AX.X, ALU.add).then_inc(row_var, 1)

            pipelined(dve, update, 5)
            dve.wait_ge(row_var, NC + SLOTS)
            dve.sem_inc(var_ready, 1)
            dve.wait_ge(std_ready, 4)
            step(dve.reciprocal(rstd, rstd))
            step(dve.tensor_tensor(rstd, rstd, inv_out[:], ALU.mult))
            scaled_rows(h2, lambda k, a, b: None)

            def split_rows():
                rows, rest = h2[:, 0:HI, :], square2[:, 0:HI, :]

                def then(ins, n):
                    ins.then_inc(split, 1)
                    dve.wait_ge(split, n)

                dve.wait_ge(iota_made, 1)
                then(dve.tensor_copy(iota_c, iota_ci), 1)
                dve.wait_ge(h_ready, 6)
                then(dve.tensor_copy(parts[:, :, 0, :], rows), 2)
                then(dve.tensor_tensor(rest, rows, parts[:, :, 0, :], ALU.subtract), 3)
                then(dve.tensor_copy(parts[:, :, 1, :], rest), 4)
                then(dve.tensor_tensor(rest, rest, parts[:, :, 1, :], ALU.subtract), 5)
                then(dve.tensor_copy(parts[:, :, 2, :], rest), 6)
                dve.wait_ge(st_h, 48)
                then(dve.memset(counts[:, 1, :, :], 0.0), 7)
                dve.sem_inc(parts_ready, 1)

            def fast_layer1():
                def next_group(d, g, slot):
                    lo = src_lo[:, bass.ds(T1 + d * TILES, TILES)].unsqueeze(2)
                    dve.tensor_tensor(hot_lo[:, slot, :, :], lo.broadcast_to([P, TILES, P]),
                                      iota_b[:, :].unsqueeze(1).broadcast_to([P, TILES, P]), ALU.is_equal).then_inc(hotlo_ready, 1)
                    dve.tensor_copy(code_s[:, slot, :], code[:, bass.ds(d * TILES, TILES)]).then_inc(staged, 1)
                    make_sel(g * TILES, slot, sel1_ready)

                def add(base, sums, width, n):
                    dve.wait_ge(table_added, n)
                    spot = table[0:D, 0, bass.ds(base, width)]
                    dve.tensor_tensor(spot, spot, sums, ALU.add).then_inc(table_added, 1)

                def place_rows(h):
                    dve.tensor_tensor(place, iota_f[0:V, 0:REACH], node_of[:, bass.ds(h, 1)].broadcast_to([V, REACH]), ALU.is_equal)

                def sum_parts(h):
                    dve.wait_ge(dense_done, h + 2)
                    dve.tensor_reduce(summed_rows, ps_t[0:V, 0:3 * D].rearrange("p (a d) -> p d a", a=3), AX.X,
                                      ALU.add).then_inc(reduced, 1)

                dve.wait_ge(agg1_done, RING)
                dve.wait_ge(count_done, CODES)
                next_group(0, 0, 0)
                with dve.Fori(0, NI1) as i:
                    for hf in range(2):
                        h = 2 * i + hf
                        base = [dve.value_load(bases[0:1, bass.ds(n, 1)], min_val=0, max_val=n_nodes)
                                for n in (2 * h + 1, 2 * h + 2, G1 + 2 * h - 3)]
                        for tile in range(HALF):
                            dve.wait_ge(count_done, h * HALF + tile + 1)
                            dve.wait_ge(staged, 2 * h + tile // TILES + 1)
                            dve.tensor_scalar(hot_code[:, tile % CODES, :], iota_c,
                                              code_s[:, tile // TILES, tile % TILES:tile % TILES + 1], None,
                                              ALU.is_equal).then_inc(code_ready, 1)
                            if tile % TILES == CODES:
                                k = tile // TILES
                                dve.wait_ge(agg1_done, 2 * h + k + RING + 1)
                                add(base[k], ps_agg[0:D, 0:WINDOW], WINDOW, 3 * h + 2 * k + 1)
                                next_group(2 * h + k + 1, 2 * h + k + 1, 1 - k)
                            if tile == CODES + 2:
                                dve.wait_ge(win_done, h + 1)
                                add(base[2], ps_win, REACH, 3 * h + 2)
                                place_rows(h)
                        sum_parts(h)
                base = [dve.value_load(bases[0:1, G1 + 2 * n + 1:G1 + 2 * n + 2], min_val=0, max_val=n_nodes)
                        for n in (NH - 2, NH - 1)]
                dve.wait_ge(win_done, NH + 1)
                add(base[0], ps_win, REACH, 3 * NH + 1)
                place_rows(NH)
                sum_parts(NH)
                dve.wait_ge(win_done, NH + 2)
                add(base[1], ps_win, REACH, 3 * NH + 2)
                dve.wait_ge(table_added, 3 * NH + 3)

            dve.wait_ge(in_ready, NC + 1)
            general = load_flag(dve, 1)
            with dve.If(general > 0):
                general_layer(1)
            with dve.Else():
                split_rows()
                fast_layer1()

            dve.wait_ge(in_root, 1)
            dve.sem_inc(edges1_done, 1)

            def finish(s, k, i, run):
                if run(0):
                    dve.wait_ge(fin_t, s + SLOTS + 1)
                    dve.reciprocal(small[:, k * CHUNK:(k + 1) * CHUNK].unsqueeze(2),
                                   ps_fin[k][:, 0:CW].rearrange("p (t c) -> p t c", c=P)[:, :, D:D + 1]).then_inc(fin_root, 1)
                if run(1):
                    b = (k + SLOTS - 1) % SLOTS
                    dve.wait_ge(fin_root, s)
                    for t in range(CHUNK):
                        row = x[:, bass.ds((s - 1) * CHUNK + t, 1), :].rearrange("p a d -> p (a d)")
                        ins = dve.scalar_tensor_tensor(row, ps_fin[b][:, t * P:t * P + D], small[:, b * CHUNK + t:b * CHUNK + t + 1], row,
                                                       ALU.mult, ALU.add)
                    ins.then_inc(fin_x, 1)

            pipelined(dve, finish, 1)

        @block.tensor
        def _(pe):
            pe.wait_ge(const_made, CONSTS)
            pe.sem_inc(pre_done, RING)
            pe.sem_inc(summed, RING)
            pe.sem_inc(agg_done, RING - 1)
            pe.sem_inc(hist_done, 2)
            pe.sem_inc(added, 2)
            pe.sem_inc(agg1_done, RING)
            pe.sem_inc(table_added, 1)
            pe.sem_inc(count_done, CODES)
            pe.sem_inc(count_copied, 2)
            pe.sem_inc(dense_done, 1)
            pe.sem_inc(nu_u, SLOTS)
            pe.sem_inc(np_t, SLOTS)
            pe.sem_inc(fin_t, SLOTS)
            pe.sem_inc(nu_y, SLOTS)
            pe.sem_inc(row_var, SLOTS)
            pe.sem_inc(fin_x, SLOTS)
            pe.sem_inc(np_tc, 1)
            pe.sem_inc(np_c, SLOTS)
            pe.sem_inc(selt_copied, 1)
            for k in range(SLOTS):
                pe.sem_inc(np_st[k], 32)
                pe.sem_inc(np_sth[k], 16)
            for L in range(2):
                pe.sem_inc(gen[L]["dstt"], 1)
                pe.sem_inc(gen[L]["hist"], 1)
                pe.sem_inc(gen[L]["free"], 1)
                pe.sem_inc(gen[L]["fold_c"], 1)
            pe.wait_ge(viol_ready, 1)
            pe.matmul(ps_t[:, 0:NG], ones[0:1, :], dst_f[0:1, 0:T:TILES], start=True, stop=True)
            pe.matmul(ps_agg[:, P:P + NH], ones[0:1, :], dst_f[0:1, T1:T:HALF], start=True, stop=True)
            for c in range(0, T - T1, 512):
                n = min(512, T - T1 - c)
                pe.matmul(ps_pre[c // 1024][:, c % 1024:c % 1024 + n], ones[0:1, :], dst_f[0:1, T1 + c:T1 + c + n],
                          start=True, stop=True)
            for j in range(HALF):
                pe.matmul(ps_deg[0:V, 0:NH], tile_row[0:1, j * V:(j + 1) * V], dst_f[0:1, T1 + j:T:HALF],
                          start=(j == 0), stop=False)
            pe.matmul(ps_deg[0:V, 0:NH], mod_row, ones[0:1, 0:1].broadcast_to([1, NH]), start=False, stop=True)
            pe.matmul(ps_deg[:, 511:512], iota_f[0:1, :], ones[0:1, 0:1], start=True, stop=True).then_inc(viol_t, 1)

            pe.wait_ge(spread, SPREADS)
            pe.wait_ge(ld_w, 16 * (10 + RING))
            pe.matmul(ps_deg[:, 256:256 + D], ones[0:1, :], ub2_r[:, :], start=True, stop=True).then_inc(bias_t, 1)

            def projection(s, k, i, run):
                if run(0):
                    pe.wait_ge(np_h, s + 1)
                    pe.wait_ge(np_tc, s + 1)
                    pe.nop(nofuse=True)
                    for t in range(CHUNK):
                        ins = pe.transpose(ps_t[0:D, t * P:(t + 1) * P], h_stage[:, k, t, :], ident[:, :])
                    ins.then_inc(np_t, 1)
                if run(1):
                    k = (k + SLOTS - 1) % SLOTS
                    pe.wait_ge(np_tc, s + 1)
                    pe.wait_ge(np_c, s)
                    for t in range(CHUNK):
                        ins = pe.matmul(ps_rows[k][:, t * 2 * H:(t + 1) * 2 * H], htc[:, k, t * P:(t + 1) * P], w1ab[:, :],
                                        start=True, stop=True)
                    ins.then_inc(np_mm, 1)

            pipelined(pe, projection, 1)
            pe.wait_ge(viol_ready, 2)
            pe.matmul(ps_deg[0:1, 0:P], small[:, 2:3], ident[:, :], start=True, stop=True)
            pe.matmul(ps_deg[0:1, P:2 * P], small[:, 15:16], ident[:, :], start=True, stop=True).then_inc(viol_t, 1)

            def open_hist():
                pe.matmul(ps_deg[:, 0:NT], ones[0:1, :], zero_r[:, 0:NT], start=True, stop=False, skip_group_check=True)

            def hist(slot, done):
                for j in range(TILES):
                    ins = pe.matmul(ps_deg[:, 0:NT], hot_lo[:, slot, j, :], hot_hi[:, slot, j, :],
                                    start=False, stop=False, skip_group_check=True)
                ins.then_inc(done, 1)

            def sel_transposed(g, slot):
                pe.wait_ge(selb_ready, g + 1)
                pe.wait_ge(selt_copied, g + 1)
                pe.nop(nofuse=True)
                for j in range(TILES):
                    ins = pe.transpose(ps_selt[0:WINDOW, j * P:(j + 1) * P], sel_b[:, slot % 2, j, :], ident_b[:, :])
                ins.then_inc(selt_done, 1)

            def products(g, q, trip):
                pe.wait_ge(ld_grp[q], 32 * trip + 32)
                pe.wait_ge(selt_copied, g + 2)
                pe.wait_ge(summed, g + RING - 1)
                for j in range(TILES):
                    ins = pe.matmul(ps_pre[q % 2][:, j * H:(j + 1) * H], lhs[0:WINDOW + De, q, j * P:(j + 1) * P],
                                    rhs[0:WINDOW + De, q, :], start=True, stop=True)
                ins.then_inc(pre_done, 1)

            def fast_layer0():
                pe.matmul(ps_sums[1][:, 0:2 * WINDOW], ones[0:1, :], zero_r[:, 0:2 * WINDOW], start=True, stop=True,
                          skip_group_check=True).then_inc(agg_done, 1)
                sel_transposed(0, 0)
                products(0, 0, 0)
                with pe.Fori(0, NI) as i:
                    for q in range(RING):
                        g = i * RING + q
                        sel_transposed(g + 1, (q + 1) % RING)
                        pe.wait_ge(hot_ready, 2 * g + 2)
                        hist(q % 2, hist_done)
                        products(g + 1, (q + 1) % RING, i + (q + 1) // RING)
                        pe.wait_ge(hid_ready, g + 1)
                        pe.wait_ge(added, g + 2)
                        for j in range(TILES):
                            for f in range(0, H, H // 2):
                                pe.matmul(ps_sums[q % 2][f:f + H // 2, 0:WINDOW], hid[:, q % 2, j, f:f + H // 2], sel[:, q, j, :],
                                          start=(j == 0), stop=(j == TILES - 1), skip_group_check=True)
                            ins = pe.matmul(ps_sums[q % 2][:, WINDOW:2 * WINDOW], ones_b[:, :], sel_b[:, q % 2, j, :],
                                            start=False, stop=(j == TILES - 1), skip_group_check=True)
                        ins.then_inc(agg_done, 1)

            def general_layer(L):
                s, width = gen[L], (H + 1, D)[L]
                val = hid[:, 0, 0:2, :].rearrange("p j f -> p (j f)") if L == 0 else gathered_h[:, 0, 0, :]
                with pe.Fori(0, NG) as g:
                    pe.wait_ge(s["ld"], (48, 32)[L] * g + (48, 32)[L])
                    if L == 0:
                        pe.wait_ge(s["hot"], 2 * g + 2)
                        hist(0, s["hist"])
                    for j in range(TILES):
                        pe.wait_ge(s["dstf"], g * TILES + j + 1)
                        pe.matmul(ps_t[:, 0:P], small[:, 4:5].broadcast_to([P, P]), ident[:, :], start=True, stop=True).then_inc(s["dstt"], 1)
                        if L == 0:
                            pe.matmul(ps_pre[0][:, 0:H], lhs[WINDOW:WINDOW + De, 0, j * P:(j + 1) * P], rhs[WINDOW:WINDOW + De, 0, :],
                                      start=True, stop=True).then_inc(s["eadot"], 1)
                        pe.wait_ge(s["sel"], (2 * TILES if L == 0 else TILES) * g + (2 if L == 0 else 1) * (j + 1))
                        pe.wait_ge(s["gat"], ((32 * TILES) if L == 0 else 16 * TILES) * g + (32 if L == 0 else 16) * (j + 1))
                        pe.matmul(ps_agg[:, 0:width], gathered[:, 1, 0, :], val[:, 0:width], start=True, stop=True).then_inc(s["comb"], 1)
                with pe.Fori(0, NT) as t:
                    pe.wait_ge(s["fold_ld"], 16 * t + 16)
                    pe.nop(nofuse=True)
                    if L == 0:
                        pe.transpose(ps_t[:, 0:P], gathered[:, 0, 0, :], ident[:, :])
                        pe.wait_ge(s["fold_diag"], t + 1)
                        pe.matmul(ps_t[:, P:2 * P], ones[:, :], gathered[:, 1, 0, :], start=True, stop=True).then_inc(s["fold_t"], 1)
                    else:
                        pe.transpose(ps_t[0:D, 0:P], gathered_h[:, 0, 0, :], ident[:, :]).then_inc(s["fold_t"], 1)

            general = load_flag(pe, 0)
            open_hist()
            with pe.If(general > 0):
                general_layer(0)
            with pe.Else():
                fast_layer0()
            pe.matmul(ps_deg[:, 0:NT], ones[0:1, :], zero_r[:, 0:NT], start=False, stop=True,
                      skip_group_check=True).then_inc(hist_closed, 1)

            def update(s, k, i, run):
                if run(0):
                    if not isinstance(s, int):
                        pe.wait_ge(nu_x, s - 2)
                    pe.matmul(ps_m[k][0:D, 0:CW], w2[:, :], table[:, 0, bass.ds(s * CW, CW)], start=True, stop=True).then_inc(nu_m, 1)
                if run(2):
                    b = (k + 1) % SLOTS
                    pe.wait_ge(nu_uc, s - 1)
                    for t in range(CHUNK):
                        for m in range(0, P, P // 2):
                            ins = pe.matmul(ps_m[b][m:m + P // 2, t * D:(t + 1) * D], utc[:, b, t * P + m:t * P + m + P // 2], u2[:, :],
                                            start=True, stop=True)
                    ins.then_inc(nu_y, 1)
                if run(1):
                    b = (k + SLOTS - 1) % SLOTS
                    pe.wait_ge(nu_ld[b], 16 * i + (16 if k else 0))
                    pe.wait_ge(nu_mc, s)
                    pe.matmul(ps_u[b][:, 0:CW], u1[:, :], cat[:, b, :], start=True, stop=True).then_inc(nu_u, 1)

            pe.wait_ge(edges_done, 1)
            pipelined(pe, update, 2)

            def fast_layer1():
                blocks = 10

                def half_product(slot, first, last):
                    for t in range(first, last):
                        ins = pe.matmul(ps_t[0:V, 0:3 * D], counts[:, slot, t, :], parts[:, t, :, :].rearrange("p a d -> p (a d)"),
                                        start=(t == 0), stop=(t == HI - 1))
                    if last == HI:
                        ins.then_inc(dense_done, 1)

                pe.wait_ge(parts_ready, 1)
                pe.matmul(ps_win, zero_r[0:1, 0:D], zero_r[0:1, 0:REACH], start=True, stop=True).then_inc(win_done, 1)
                with pe.Fori(0, NI1) as i:
                    for hf in range(2):
                        h = 2 * i + hf
                        for tile in range(HALF):
                            if tile % TILES == 0:
                                k = tile // TILES
                                q = 2 * hf + k
                                pe.wait_ge(sel1_ready, 2 * h + k + 1)
                                pe.wait_ge(gat1[q], 16 * TILES * i + 16 * TILES)
                                pe.wait_ge(table_added, 3 * h + 2 * k + 1 - k)
                                for j in range(TILES):
                                    ins = pe.matmul(ps_agg[0:D, 0:WINDOW], ring1[:, q, j, :], sel[:, k, j, :],
                                                    start=(j == 0), stop=(j == TILES - 1))
                                ins.then_inc(agg1_done, 1)
                                pe.wait_ge(hotlo_ready, 2 * h + k + 1)
                            pe.wait_ge(code_ready, h * HALF + tile + 1)
                            pe.wait_ge(count_copied, h * HALF + tile + 1)
                            for b in range(2):
                                w = HI // 2 * SPAN
                                ins = pe.matmul(ps_pre[tile % 2][:, 512 * b:512 * b + w], hot_lo[:, tile // TILES, tile % TILES, :],
                                                hot_code[:, tile % CODES, b * w:(b + 1) * w], start=True, stop=True)
                            ins.then_inc(count_done, 1)
                            if tile == 1:
                                pe.wait_ge(count_copied, h * HALF + 2)
                            if 1 <= tile <= blocks:
                                half_product(1 - hf, HI * (tile - 1) // blocks, HI * tile // blocks)
                        pe.wait_ge(reduced, h + 1)
                        pe.wait_ge(table_added, 3 * h + 3)
                        pe.matmul(ps_win, summed_rows, place, start=True, stop=True).then_inc(win_done, 1)
                pe.wait_ge(count_copied, NH * HALF + 2)
                half_product(1, 0, HI)
                pe.wait_ge(reduced, NH + 1)
                pe.wait_ge(table_added, 3 * NH + 2)
                pe.matmul(ps_win, summed_rows, place, start=True, stop=True).then_inc(win_done, 1)

            pe.wait_ge(in_ready, NC + 1)
            general = load_flag(pe, 1)
            with pe.If(general > 0):
                general_layer(1)
            with pe.Else():
                fast_layer1()
            pe.wait_ge(edges1_done, 1)
            with pe.Fori(0, NCH) as i:
                for k in range(SLOTS):
                    c = i * SLOTS + k
                    pe.wait_ge(fin_staged, c + 1)
                    pe.wait_ge(fin_x, c + 1)
                    pe.nop(nofuse=True)
                    for t in range(CHUNK):
                        ins = pe.transpose(ps_fin[k][:, t * P:(t + 1) * P], fin_stage[:, k, t * P:(t + 1) * P], ident[:, :])
                    ins.then_inc(fin_t, 1)


_OUT = "out_dram"


def kernel(x, src, dst, edge_attr_32, L0_gnn_mW1, L0_gnn_mb1, L0_gnn_mW2, L0_gnn_mb2, L0_gnn_uW1, L0_gnn_ub1,
           L0_gnn_uW2, L0_gnn_ub2):
    import concourse.bacc as bacc
    from concourse.bass_utils import run_bass_kernel_spmd

    x, src, dst, ea = (np.asarray(a) for a in (x, src, dst, edge_attr_32))
    n, d = x.shape
    e, de = ea.shape
    nt, ng = padded_sizes(n, e)
    x_t = np.zeros((nt * P, d), x.dtype)
    x_t[:n] = x
    x_t = np.ascontiguousarray(x_t.reshape(nt, P, d).transpose(1, 0, 2))

    def columns(a):
        p = np.full(ng * GROUP, n, a.dtype)
        p[:e] = a
        return np.ascontiguousarray(p.reshape(ng * TILES, P).T)

    ea_t = np.zeros((de, (ng + 1) * GROUP), ea.dtype)
    ea_t[:, :e] = ea.T
    arrays = {"x_t": x_t, "src_t": columns(src), "dst_t": columns(dst), "ea_t": ea_t}
    for name, w in (("mW1", L0_gnn_mW1), ("mb1", L0_gnn_mb1), ("mW2", L0_gnn_mW2), ("mb2", L0_gnn_mb2),
                    ("uW1", L0_gnn_uW1), ("ub1", L0_gnn_ub1), ("uW2", L0_gnn_uW2), ("ub2", L0_gnn_ub2)):
        arrays[name] = np.ascontiguousarray(w)
    nc = bacc.Bacc("TRN2", target_bir_lowering=False, num_devices=1)
    args = [nc.dram_tensor(k, a.shape, mybir.dt.from_np(a.dtype), kind="ExternalInput").ap() for k, a in arrays.items()]
    out = nc.dram_tensor(_OUT, x_t.shape, F32, kind="ExternalOutput").ap()
    bass_preln_mpnn_lightgcn(nc, *args, out, n, e)
    got = run_bass_kernel_spmd(nc, [arrays], core_ids=[0]).results[0][_OUT]
    return got.transpose(1, 0, 2).reshape(nt * P, d)[:n]
```
